# Optimizing a Trainium2 kernel written in Bass

```python
import numpy as np
import jax
import jax.numpy as jnp

def _softmax(x, axis=-1):
    return jax.nn.softmax(x, axis=axis)

def _gelu(x):
    return jax.nn.gelu(x, approximate=True)

def _silu(x):
    return jax.nn.silu(x)

def _sigmoid(x):
    return jax.nn.sigmoid(x)

def _layernorm(x, axis=-1, eps=1e-05):
    m = jnp.mean(x, axis=axis, keepdims=True)
    v = jnp.var(x, axis=axis, keepdims=True)
    return (x - m) / jnp.sqrt(v + eps)

def _scatter_add(tgt, idx, src, axis=0):
    return tgt.at[idx].add(src)

def _segment_sum(src, seg, n):
    return jax.ops.segment_sum(src, seg, n)
kernel_name = 'mk_adaln_d1_jaxref_r8_12d09b'

def setup_inputs(seed: int=0):
    np.random.seed(seed)
    _w = jnp.asarray

    def _L0_attn_setup():
        import jax, jax.numpy as jnp
        import numpy as np
        B, T, C, H = (4, 256, 128, 16)
        INIT_STD = 0.02
        key = jax.random.key(seed)
        ks = jax.random.split(key, 9)
        x = jax.random.normal(ks[0], (B, T, C), dtype=jnp.float32)

        def dense(kw):
            return jax.random.normal(kw, (C, C), dtype=jnp.float32) * INIT_STD
        return {'x': x, 'Wq': dense(ks[1]), 'bq': jnp.zeros((C,), jnp.float32), 'Wk': dense(ks[2]), 'bk': jnp.zeros((C,), jnp.float32), 'Wv': dense(ks[3]), 'bv': jnp.zeros((C,), jnp.float32), 'Wo': dense(ks[4]), 'bo': jnp.zeros((C,), jnp.float32)}
    _L0_attn_in = _L0_attn_setup()

    def _L0_ffn_setup():
        import jax, jax.numpy as jnp
        import numpy as np
        D = 128
        H = 16
        DK = D // H
        E = 8
        DFF = 4 * D
        TOPK = 2
        EPS = 1e-05

        def _layernorm(x, g, b):
            m = jnp.mean(x, axis=-1, keepdims=True)
            v = jnp.mean(jnp.square(x - m), axis=-1, keepdims=True)
            return (x - m) * jax.lax.rsqrt(v + EPS) * g + b
        key = jax.random.key(seed)
        ks = jax.random.split(key, 16)
        s_in = 1.0 / np.sqrt(D)
        s_ff = 1.0 / np.sqrt(DFF)
        return {'x': jax.random.normal(ks[0], (2, 256, D), dtype=jnp.float32), 'ln1_g': jnp.ones((D,), jnp.float32), 'ln1_b': jnp.zeros((D,), jnp.float32), 'w_qkv': jax.random.normal(ks[1], (D, 3 * D), jnp.float32) * s_in, 'b_qkv': jnp.zeros((3 * D,), jnp.float32), 'w_o': jax.random.normal(ks[2], (D, D), jnp.float32) * s_in, 'b_o': jnp.zeros((D,), jnp.float32), 'ln2_g': jnp.ones((D,), jnp.float32), 'ln2_b': jnp.zeros((D,), jnp.float32), 'gate_w': jax.random.normal(ks[3], (D, E), jnp.float32) * s_in, 'gate_b': jnp.zeros((E,), jnp.float32), 'W1': jax.random.normal(ks[4], (E, D, DFF), jnp.float32) * s_in, 'b1': jnp.zeros((E, DFF), jnp.float32), 'W2': jax.random.normal(ks[5], (E, DFF, D), jnp.float32) * s_ff, 'b2': jnp.zeros((E, D), jnp.float32)}
    _L0_ffn_in = _L0_ffn_setup()
    _L0_c = _w((lambda *s: np.random.randn(*s).astype(np.float32) * 0.05)(8, 128))
    _L0_wmod = _w((lambda *s: np.random.randn(*s).astype(np.float32) * 0.05)(128, 6 * 128) * 128 ** (-0.5))
    _d = {'L0_attn_x': _L0_attn_in['x'], 'L0_attn_Wq': _L0_attn_in['Wq'], 'L0_attn_bq': _L0_attn_in['bq'], 'L0_attn_Wk': _L0_attn_in['Wk'], 'L0_attn_bk': _L0_attn_in['bk'], 'L0_attn_Wv': _L0_attn_in['Wv'], 'L0_attn_bv': _L0_attn_in['bv'], 'L0_attn_Wo': _L0_attn_in['Wo'], 'L0_attn_bo': _L0_attn_in['bo'], 'L0_ffn_ln1_g': _L0_ffn_in['ln1_g'], 'L0_ffn_ln1_b': _L0_ffn_in['ln1_b'], 'L0_ffn_w_qkv': _L0_ffn_in['w_qkv'], 'L0_ffn_b_qkv': _L0_ffn_in['b_qkv'], 'L0_ffn_w_o': _L0_ffn_in['w_o'], 'L0_ffn_b_o': _L0_ffn_in['b_o'], 'L0_ffn_ln2_g': _L0_ffn_in['ln2_g'], 'L0_ffn_ln2_b': _L0_ffn_in['ln2_b'], 'L0_ffn_gate_w': _L0_ffn_in['gate_w'], 'L0_ffn_gate_b': _L0_ffn_in['gate_b'], 'L0_ffn_W1': _L0_ffn_in['W1'], 'L0_ffn_b1': _L0_ffn_in['b1'], 'L0_ffn_W2': _L0_ffn_in['W2'], 'L0_ffn_b2': _L0_ffn_in['b2'], 'L0_c': _L0_c, 'L0_wmod': _L0_wmod}
    _x0 = _d['L0_attn_x']
    _d['L0_attn_x'] = jax.random.normal(jax.random.fold_in(jax.random.key(seed), 1), (8, 256, 128), dtype=_x0.dtype)
    del _x0
    return _d

def reference(L0_attn_x, L0_attn_Wq, L0_attn_bq, L0_attn_Wk, L0_attn_bk, L0_attn_Wv, L0_attn_bv, L0_attn_Wo, L0_attn_bo, L0_ffn_ln1_g, L0_ffn_ln1_b, L0_ffn_w_qkv, L0_ffn_b_qkv, L0_ffn_w_o, L0_ffn_b_o, L0_ffn_ln2_g, L0_ffn_ln2_b, L0_ffn_gate_w, L0_ffn_gate_b, L0_ffn_W1, L0_ffn_b1, L0_ffn_W2, L0_ffn_b2, L0_c, L0_wmod):

    def _L0_attn_ref(x, Wq, bq, Wk, bk, Wv, bv, Wo, bo):
        import jax, jax.numpy as jnp
        import numpy as np
        B, T, C, H = (4, 256, 128, 16)
        INIT_STD = 0.02
        b, t, c = x.shape
        hd = c // H

        def split_heads(y):
            return jnp.transpose(y.reshape(b, t, H, hd), (0, 2, 1, 3))
        q = split_heads(x @ Wq + bq)
        k = split_heads(x @ Wk + bk)
        v = split_heads(x @ Wv + bv)
        scale = 1.0 / jnp.sqrt(jnp.float32(hd))
        att = jnp.einsum('bhqd,bhkd->bhqk', q, k) * scale
        mask = jnp.tril(jnp.ones((t, t), dtype=bool))[None, None]
        att = jnp.where(mask, att, jnp.float32(-jnp.inf))
        att = jax.nn.softmax(att, axis=-1)
        y = jnp.einsum('bhqk,bhkd->bhqd', att, v)
        y = jnp.transpose(y, (0, 2, 1, 3)).reshape(b, t, c)
        return y @ Wo + bo

    def _L0_ffn_ref(x, ln1_g, ln1_b, w_qkv, b_qkv, w_o, b_o, ln2_g, ln2_b, gate_w, gate_b, W1, b1, W2, b2):
        import jax, jax.numpy as jnp
        import numpy as np
        D = 128
        H = 16
        DK = D // H
        E = 8
        DFF = 4 * D
        TOPK = 2
        EPS = 1e-05

        def _layernorm(x, g, b):
            m = jnp.mean(x, axis=-1, keepdims=True)
            v = jnp.mean(jnp.square(x - m), axis=-1, keepdims=True)
            return (x - m) * jax.lax.rsqrt(v + EPS) * g + b
        B, S, _ = x.shape
        h = _layernorm(x, ln1_g, ln1_b)
        qkv = h @ w_qkv + b_qkv
        q, k, v = jnp.split(qkv, 3, axis=-1)
        q = q.reshape(B, S, H, DK)
        k = k.reshape(B, S, H, DK)
        v = v.reshape(B, S, H, DK)
        scores = jnp.einsum('bqhd,bkhd->bhqk', q, k) / np.sqrt(DK)
        attn = jax.nn.softmax(scores, axis=-1)
        o = jnp.einsum('bhqk,bkhd->bqhd', attn, v).reshape(B, S, D)
        x = x + o @ w_o + b_o
        h = _layernorm(x, ln2_g, ln2_b).reshape(B * S, D)
        logits = h @ gate_w + gate_b
        topv, topi = jax.lax.top_k(logits, TOPK)
        gw = jax.nn.softmax(topv, axis=-1)
        ew = jnp.sum(jax.nn.one_hot(topi, E, dtype=h.dtype) * gw[..., None], axis=1)
        hid = jax.nn.relu(jnp.einsum('td,edf->etf', h, W1) + b1[:, None, :])
        out_e = jnp.einsum('etf,efd->etd', hid, W2) + b2[:, None, :]
        moe = jnp.einsum('etd,te->td', out_e, ew)
        return x + moe.reshape(B, S, D)
    x = L0_attn_x
    mod = (_silu(L0_c) @ L0_wmod).reshape(L0_c.shape[0], 6, 1, -1)
    sa, ca, ga, sb, cb, gb = (mod[:, 0], mod[:, 1], mod[:, 2], mod[:, 3], mod[:, 4], mod[:, 5])
    ga = (2 * (ga >= 0) - 1) * jnp.maximum(jnp.abs(ga), 0.25)
    gb = (2 * (gb >= 0) - 1) * jnp.maximum(jnp.abs(gb), 0.25)
    h = _layernorm(x, axis=-1) * (1 + ca) + sa
    x = x + ga * _L0_attn_ref(h, L0_attn_Wq, L0_attn_bq, L0_attn_Wk, L0_attn_bk, L0_attn_Wv, L0_attn_bv, L0_attn_Wo, L0_attn_bo)
    h = _layernorm(x, axis=-1) * (1 + cb) + sb
    x = x + gb * _L0_ffn_ref(h, L0_ffn_ln1_g, L0_ffn_ln1_b, L0_ffn_w_qkv, L0_ffn_b_qkv, L0_ffn_w_o, L0_ffn_b_o, L0_ffn_ln2_g, L0_ffn_ln2_b, L0_ffn_gate_w, L0_ffn_gate_b, L0_ffn_W1, L0_ffn_b1, L0_ffn_W2, L0_ffn_b2)
    return x

_drawn_inputs = setup_inputs


def setup_inputs(seed=0):
    import zlib

    import numpy as np

    out = dict(_drawn_inputs(seed))
    spreads = {'L0_attn_bq': (0.0, 0.8),
     'L0_attn_bk': (0.0, 0.8),
     'L0_attn_bv': (0.0, 0.745),
     'L0_attn_bo': (0.0, 0.1),
     'L0_ffn_ln1_g': (1.0, 0.2),
     'L0_ffn_ln1_b': (0.0, 0.1),
     'L0_ffn_b_qkv': (0.0, 0.1),
     'L0_ffn_b_o': (0.0, 0.1),
     'L0_ffn_ln2_g': (1.0, 0.2),
     'L0_ffn_ln2_b': (0.0, 0.1),
     'L0_ffn_gate_b': (0.0, 0.1),
     'L0_ffn_b1': (0.0, 0.642),
     'L0_ffn_b2': (0.0, 0.454)}
    factors = {'L0_attn_Wq': 8.0, 'L0_attn_Wk': 8.0, 'L0_attn_Wv': 8.0, 'L0_attn_Wo': 5.814}
    for name, (base, spread) in spreads.items():
        noise = np.random.default_rng([zlib.crc32(name.encode()), seed]).standard_normal(out[name].shape)
        drawn = base * np.exp(spread * noise) if base else spread * noise
        out[name] = jnp.asarray(drawn.astype(out[name].dtype))
    for name, factor in factors.items():
        out[name] = (out[name] * factor).astype(out[name].dtype)
    return out
```

```python
from contextlib import ExitStack

import concourse.bass as bass
from concourse import mybir

F32 = mybir.dt.float32
BF16 = mybir.dt.bfloat16
U32 = mybir.dt.uint32
ALU = mybir.AluOpType
ACT = mybir.ActivationFunctionType
AX = mybir.AxisListType

P = 128
HD = 8
HEADS = 16
GH = 4
GROUPS = HEADS // GH
SLOTS = HEADS // 2
QROWS = 6 * HD
SROWS = QROWS + 2
VW = 32
TURNS = 2 * GROUPS
EPS = 1e-5
SCALE = HD ** -0.5
MASKED = -1e30
TOPK_W = 8
PAIRS = [(0, 0), (0, 1), (0, 2), (1, 0), (1, 1), (2, 0)]
SA, CA, GA, SB_, CB, GB = range(6)
PARAMS = 23
CONSTS = 9
SETUP_SILU, SETUP_MOD = 4, 11
TOP_DIF, TOP_ALL = 2, 11


def at_least(eng, sem, value):
    if isinstance(value, int) and value <= 0:
        return
    eng.wait_ge(sem, value)


def build(nc, io, out, mod_dram):
    x_dram = io["L0_attn_x"]
    B, T, C = x_dram.shape
    E = io["L0_ffn_gate_w"].shape[1]
    DFF = io["L0_ffn_W1"].shape[2]
    NJ = DFF // P
    NT = T // P
    TILES = B * NT
    LOOP = (3, B - 1)
    assert C == P and NT == 2 and T == 256

    def live(b):
        return not isinstance(b, int) or 0 <= b < B

    def group_at(i, turn):
        if turn < 0:
            i, turn = i - 1, turn + TURNS
        if turn >= TURNS:
            i, turn = i + 1, turn - TURNS
        k = turn // 2
        if turn % 2 == 0:
            return 0, i, k
        return 1, i - 2, k

    def place_of(L, b, g):
        if L == 0:
            return 4 * b + g if isinstance(b, int) and b < 2 else 8 * b + 2 * g - 8
        if isinstance(b, int) and b >= B - 2:
            return 8 * (B - 1) + 4 * (b - (B - 2)) + g
        return 8 * b + 2 * g + 9

    def probs_of(L, b, g):
        n = place_of(L, b, g)
        return n % 2 if isinstance(n, int) else L

    def bank_uses(L, i):
        if L == 0:
            order = [("yT", i - 1, 3), ("y2T", i - 1, 0), ("wo", i - 1, 0), ("xT", i + 1, 0), ("yT", i, 0),
                     ("qk", i + 1, 0), ("v", i + 1, 0), ("yT", i, 1), ("yT", i, 2)]
        else:
            order = [("yT", i - 3, 3), ("y2T", i - 3, 0), ("wo", i - 3, 0), ("yT", i - 2, 0), ("h3T", i - 3, 0),
                     ("xT", i - 1, 0), ("gate", i - 3, 0), ("qk", i - 1, 0), ("v", i - 1, 0), ("yT", i - 2, 1),
                     ("yT", i - 2, 2)]
        return [u for u in order if live(u[1])]

    def bank_place(L, i, what, g=0):
        n = i if isinstance(i, int) else LOOP[0]
        before = sum(len(bank_uses(L, m)) for m in range(-1, n))
        names = [(u[0], u[2]) for u in bank_uses(L, n)]
        here = before + names.index((what, g)) + 1
        if isinstance(i, int):
            return here
        return (i - LOOP[0]) * len(bank_uses(L, n)) + here

    ctx = ExitStack()
    with ctx:
        def sb(name, shape, dt=F32):
            return ctx.enter_context(nc.sbuf_tensor(name, shape, dt))

        def pb(name, shape, dt=F32):
            return ctx.enter_context(nc.psum_tensor(name, shape, dt))

        def sem(name):
            return ctx.enter_context(nc.semaphore(name))

        def sems(name):
            return [sem(f"{name}{L}") for L in range(2)]

        w_in = [sb("w_in0", [P, 3 * C]), sb("w_in1", [P, 3 * C])]
        w_qk = [sb(f"w_qk{L}", [P, 2, C]) for L in range(2)]
        w_out = [sb("w_out0", [P, C]), sb("w_out1", [P, C])]
        gate_w = sb("gate_w", [P, E])
        wmod = sb("wmod", [P, 6 * C])
        c_rows = sb("c_rows", [B, C])
        qk_rows = sb("qk_rows", [4, C])
        qk_rows_p = sb("qk_rows_p", [4, C])
        NV = 6
        vec_rows = sb("vec_rows", [NV + E * NJ, C])
        qk_bias = sb("qk_bias", [P, 4])
        vec = sb("vec", [P, NV + E * NJ])
        BV0, BV1, G1, B1_, G2, B2_ = range(NV)
        b2_rows = sb("b2_rows", [E, C])
        gate_b = sb("gate_b", [P, E])
        bo_bc = [sb("bo_bc0", [P, C]), sb("bo_bc1", [P, C])]
        ident = sb("ident", [P, P])
        ident_bf = sb("ident_bf", [P, P], BF16)
        zeros = sb("zeros", [P, P])
        mask_qk = sb("mask_qk", [P, P], BF16)
        mask_kq = sb("mask_kq", [P, P], BF16)
        eps = sb("eps", [P, NT])
        minus_half = sb("minus_half", [P, NT])
        silu_e = sb("silu_e", [B, C])
        silu_r = sb("silu_r", [B, C])
        silu_c = sb("silu_c", [B, C])
        silu_cT = sb("silu_cT", [P, B])
        mod = sb("mod", [B, 6, C])
        mod_sign = sb("mod_sign", [B, 2, C])
        mod_abs = sb("mod_abs", [B, 2, C])

        x_in = sb("x_in", [P, NT, C])
        x_res = sb("x_res", [P, NT, C])
        mod_a = sb("mod_a", [P, 2, C])
        ga_bc = sb("ga_bc", [P, C])
        mod_b = sb("mod_b", [P, 2, C])
        gabo = sb("gabo", [P, C])
        x_gabo = sb("x_gabo", [P, NT, C])
        attn_g = sb("attn_g", [P, NT, C])
        x1 = sb("x1", [P, NT, C])
        xf = sb("xf", [P, NT, C])
        xf2 = sb("xf2", [P, NT, C])
        stats = sb("stats", [P, 4, NT, 6])
        mean_var = sb("mean_var", [P, 4, NT, 2])
        var_eps = sb("var_eps", [P, 4, NT])
        rstd = sb("rstd", [P, 4, NT])
        xn = [sb(f"xn{n}", [P, NT, C]) for n in range(4)]
        xm = [sb(f"xm{n}", [P, NT, C]) for n in range(2)]
        h_a = sb("h_a", [P, NT, C])
        hT = [sb(f"hT{L}", [P, T]) for L in range(2)]
        parts = [sb(f"parts{L}", [P, 6, T], BF16) for L in range(2)]
        rest = [sb(f"rest{L}", [P, 2, T]) for L in range(2)]
        stacked = [sb(f"stacked{L}", [P, SLOTS, 2, T], BF16) for L in range(2)]
        ones_bf = sb("ones_bf", [2, SLOTS, T], BF16)
        v_flat = [sb(f"v_flat{L}", [P, NT, C]) for L in range(2)]
        v_pad = [sb(f"v_pad{L}", [P, NT, HEADS, VW]) for L in range(2)]
        neg_max = [sb("neg_max0", [P, 3, GH]), sb("neg_max1", [P, 2, GH])]
        max_parts = [sb(f"max_parts{L}", [P, NT, 2, GH], BF16) for L in range(2)]
        max_rows = sb("max_rows", [2 * GH, T], BF16)
        probs = [sb(f"probs{n}", [P, GH, NT, T]) for n in range(2)]
        y_sb = [sb(f"y_sb{L}", [P, T]) for L in range(2)]
        y_inv = [sb(f"y_inv{L}", [P, NT, GH, 1]) for L in range(2)]
        y_norm = [sb(f"y_norm{L}", [P, NT, HEADS, HD]) for L in range(2)]
        yT = [sb(f"yT{L}", [P, T]) for L in range(2)]
        h3 = sb("h3", [P, T])

        X1 = sb("X1", [P, TILES, C])
        XF = sb("XF", [P, TILES, C])
        H3 = sb("H3", [P, TILES * P])
        LG = sb("LG", [P, TILES, E])
        GBC = sb("GBC", [P, B, C])

        top = sb("top", [P, TILES, TOPK_W])
        top_i = sb("top_i", [P, TILES, TOPK_W], U32)
        top_f = sb("top_f", [P, TILES, 2])
        iota_e = sb("iota_e", [P, E])
        t_dif = sb("t_dif", [P, TILES, 1])
        t_exp = sb("t_exp", [P, TILES, 1])
        t_sum = sb("t_sum", [P, TILES, 1])
        w_top = sb("w_top", [P, 2, TILES, 1])
        pick = sb("pick", [P, 2, TILES, E])
        EW = sb("EW", [P, TILES, E])
        ewT = sb("ewT", [E, TILES * P])
        ew_e = [sb(f"ew_e{n}", [P, TILES]) for n in range(2)]
        b1_e = [sb(f"b1_e{n}", [P, NJ]) for n in range(2)]
        W1 = [sb(f"W1_{n}", [P, DFF]) for n in range(2)]
        W2 = [sb(f"W2_{n}", [P, NJ, C]) for n in range(2)]
        NCH = TILES * P // 512
        hid = [sb(f"hid{n}", [P, NJ, 512]) for n in range(2)]

        bank = [pb(f"bank{n}", [P, 512]) for n in range(8)]
        row_bank, col_bank, av_bank, max_bank = bank[0:2], bank[2:4], bank[4], bank[5]
        small = bank[6:8]
        max_rows_ps = max_bank[:, :].bitcast(BF16)

        params_in = sem("params_in")
        consts = sem("consts")
        dve_setup = sem("dve_setup")
        act_setup = sem("act_setup")
        pe_setup = sem("pe_setup")
        pool_setup = sem("pool_setup")
        mod_out = sem("mod_out")
        passed = sem("passed")
        x_in_landed = sem("x_in_landed")
        x_res_landed = sem("x_res_landed")
        mod_b_landed = sem("mod_b_landed")
        stats_done = [sem(f"stats_done{n}") for n in range(4)]
        aggr_done = [sem(f"aggr_done{n}") for n in range(4)]
        eps_done = [sem(f"eps_done{n}") for n in range(4)]
        rstd_done = [sem(f"rstd_done{n}") for n in range(4)]
        norm_done = [sem(f"norm_done{n}") for n in range(4)]
        scale_done = [sem(f"scale_done{n}") for n in range(2)]
        shift_done = [sem(f"shift_done{n}") for n in range(2)]
        high_done = sems("high_done")
        mid_done = sems("mid_done")
        low_done = sems("low_done")
        half_landed = [sems(f"half{h}_landed") for h in range(2)]
        v_half_done = [sems(f"v_half{h}_done") for h in range(2)]
        small_full = sems("small_full")
        small_free = sems("small_free")
        rows_full = sem("rows_full")
        rows_free = sem("rows_free")
        cols_full = sem("cols_full")
        cols_free = sem("cols_free")
        max_split = sems("max_split")
        max_step = sems("max_step")
        maxT_full = sem("maxT_full")
        maxT_free = sem("maxT_free")
        shift_landed = sem("shift_landed")
        av_full = sem("av_full")
        y_sb_done = sem("y_sb_done")
        inv_done = sems("inv_done")
        y_norm_done = sems("y_norm_done")
        gabo_done = sem("gabo_done")
        x_gabo_done = sem("x_gabo_done")
        x1_done = sem("x1_done")
        x1_kept = sem("x1_kept")
        xf_kept = sem("xf_kept")
        xf2_free = sem("xf2_free")
        h3_free = sem("h3_free")
        gb_landed = sem("gb_landed")
        top_step = sem("top_step")
        ew_exp = sem("ew_exp")
        ewT_full = sem("ewT_full")
        ewT_done = sem("ewT_done")
        b2_full = sem("b2_full")
        b2_added = sem("b2_added")
        w_landed = [sem(f"w_landed{n}") for n in range(2)]
        cols_e = sem("cols_e")
        up_full = sem("up_full")
        relu_done = sem("relu_done")
        down_full = sem("down_full")
        acc_done = sem("acc_done")
        gated = sem("gated")
        final = sem("final")
        stored = sem("stored")

        half_rows = [slice(64 * h, 64 * h + QROWS) for h in range(2)]
        x_v = x_dram.rearrange("b (t p) c -> b p t c", p=P)
        out_v = out.rearrange("b (t p) c -> p (b t) c", p=P)
        w1_v = io["L0_ffn_W1"]
        w2_v = io["L0_ffn_W2"].rearrange("e (j p) c -> e p j c", p=P)
        EXPERT_LOOP = E // 2

        def row(v):
            return v.rearrange("(o c) -> o c", o=1)

        def bcast(ap, n=NT):
            return ap[:, None, :].to_broadcast([P, n, C])

        def over_iterations(eng, body):
            for i in range(-1, LOOP[0]):
                body(i)
            with eng.Fori(LOOP[0], LOOP[1]) as i:
                body(i)
            for i in range(LOOP[1], B + 3):
                body(i)

        def over_experts(eng, body):
            body(0)
            with eng.Fori(1, EXPERT_LOOP) as m:
                body(m)

        block = ctx.enter_context(nc.Block())

        @block.sync
        def _(sp):
            loads = [
                (c_rows[:, :], io["L0_c"]), (wmod[:, :], io["L0_wmod"]),
                (w_in[0][:, 0:C], io["L0_attn_Wq"]), (w_in[0][:, C:2 * C], io["L0_attn_Wk"]),
                (w_in[0][:, 2 * C:3 * C], io["L0_attn_Wv"]), (w_in[1][:, :], io["L0_ffn_w_qkv"]),
                (w_out[0][:, :], io["L0_attn_Wo"]), (w_out[1][:, :], io["L0_ffn_w_o"]),
                (gate_w[:, :], io["L0_ffn_gate_w"]),
                (qk_rows[0:1, :], row(io["L0_attn_bq"])), (qk_rows[1:2, :], row(io["L0_attn_bk"])),
                (qk_rows[2:4, :], io["L0_ffn_b_qkv"][0:2 * C].rearrange("(r c) -> r c", r=2)),
                (vec_rows[BV0:BV0 + 1, :], row(io["L0_attn_bv"])),
                (vec_rows[BV1:BV1 + 1, :], row(io["L0_ffn_b_qkv"][2 * C:3 * C])),
                (vec_rows[G1:G1 + 1, :], row(io["L0_ffn_ln1_g"])), (vec_rows[B1_:B1_ + 1, :], row(io["L0_ffn_ln1_b"])),
                (vec_rows[G2:G2 + 1, :], row(io["L0_ffn_ln2_g"])), (vec_rows[B2_:B2_ + 1, :], row(io["L0_ffn_ln2_b"])),
                (vec_rows[NV:NV + E * NJ, :], io["L0_ffn_b1"].rearrange("e (j p) -> (e j) p", p=P)),
                (b2_rows[:, :], io["L0_ffn_b2"]),
                (gate_b[:, :], row(io["L0_ffn_gate_b"]).to_broadcast([P, E])),
                (bo_bc[0][:, :], row(io["L0_attn_bo"]).to_broadcast([P, C])),
                (bo_bc[1][:, :], row(io["L0_ffn_b_o"]).to_broadcast([P, C])),
            ]
            for dst, src in loads:
                sp.dma_start(dst, src).then_inc(params_in, 16)
            assert len(loads) == PARAMS
            sp.wait_ge(consts, CONSTS)
            for L in range(2):
                for h in range(2):
                    sp.dma_start(stacked[L][64 * h + QROWS:64 * h + SROWS, :, 1, :], ones_bf[:, :, :]).then_inc(half_landed[h][L], 16)
            sp.wait_ge(dve_setup, SETUP_MOD)
            sp.dma_start(mod_dram, mod[:, :, :].rearrange("b m c -> b (m c)")).then_inc(mod_out, 16)
            sp.wait_ge(mod_out, 16)
            for b in range(B):
                sp.dma_start(GBC[:, b, :], mod_dram[b:b + 1, GB * C:(GB + 1) * C].to_broadcast([P, C])).then_inc(gb_landed, 16)

            def mod_row(b, m, n):
                return mod_dram[bass.ds(b, 1), m * C:(m + n) * C].to_broadcast([P, n * C])

            def load_x(b):
                at_least(sp, shift_done[0], b)
                sp.dma_start(x_in[:, :, :], x_v[bass.ds(b, 1)].rearrange("o p t c -> (o p) t c")).then_inc(x_in_landed, 16)
                sp.dma_start(mod_a[:, :, :].rearrange("p m c -> p (m c)"), mod_row(b, SA, 2)).then_inc(x_in_landed, 16)

            def load_res(b):
                at_least(sp, x_gabo_done, b)
                at_least(sp, x1_done, b)
                sp.dma_start(x_res[:, :, :], x_v[bass.ds(b, 1)].rearrange("o p t c -> (o p) t c")).then_inc(x_res_landed, 16)
                sp.dma_start(ga_bc[:, :], mod_row(b, GA, 1)).then_inc(x_res_landed, 16)

            def load_mod_b(b):
                at_least(sp, shift_done[1], b)
                sp.dma_start(mod_b[:, :, :].rearrange("p m c -> p (m c)"), mod_row(b, SB_, 2)).then_inc(mod_b_landed, 16)

            def stack(L, b, h):
                at_least(sp, low_done[L], b + 1)
                if not isinstance(b, int) or b > 0:
                    sp.wait_ge(cols_full, 4 * place_of(L, b - 1, 2 * h + 1) + 4)
                for n, (qp, kp) in enumerate(PAIRS):
                    src = parts[L][64 * h:64 * h + 64, qp:4 + kp:3 + kp - qp, :]
                    dst = stacked[L][64 * h + HD * n:64 * h + HD * (n + 1), :, :, :]
                    sp.dma_start(dst, src).then_inc(half_landed[h][L], 16)

            def body(i):
                for turn in range(TURNS):
                    if turn == 0 and live(i + 1):
                        load_x(i + 1)
                    if turn == 1 and live(i):
                        load_res(i)
                    if turn == 3 and live(i + 1):
                        stack(0, i + 1, 0)
                    if turn == 5 and live(i - 1):
                        stack(1, i - 1, 0)
                    if turn == 6 and live(i + 1):
                        stack(0, i + 1, 1)
                    if turn == 7 and live(i):
                        load_mod_b(i)
                    if turn == 7 and live(i - 1):
                        stack(1, i - 1, 1)

            over_iterations(sp, body)

            def load_experts(m):
                for n in range(2):
                    at_least(sp, down_full, (m * 2 + n - 1) * NCH)
                    sp.dma_start(W1[n][:, :], w1_v[bass.ds(m * 2 + n, 1)].rearrange("o p f -> (o p) f")).then_inc(w_landed[n], 16)
                    sp.dma_start(W2[n][:, :, :], w2_v[bass.ds(m * 2 + n, 1)].rearrange("o p j c -> (o p) j c")).then_inc(w_landed[n], 16)
            over_experts(sp, load_experts)
            for ch in range(NCH):
                sp.wait_ge(final, ch + 1)
                sp.dma_start(out_v[:, 4 * ch:4 * ch + 4, :], X1[:, 4 * ch:4 * ch + 4, :]).then_inc(stored, 16)
            sp.wait_ge(stored, 16 * NCH)

        @block.gpsimd
        def _(pool):
            pool.memset(zeros[:, :], 0.0).then_inc(pool_setup, 1)
            pool.memset(eps[:, :], EPS).then_inc(consts, 1)
            pool.memset(minus_half[:, :], -0.5).then_inc(consts, 1)
            pool.memset(ones_bf[:, :, :], 1.0).then_inc(consts, 1)
            pool.iota(iota_e[:, :], pattern=[[1, E]], base=0, channel_multiplier=0,
                      allow_small_or_imprecise_dtypes=True).then_inc(consts, 1)
            for L in range(2):
                pool.memset(v_pad[L][:, :, :, :], 0.0).then_inc(pool_setup, 1)
            pool.wait_ge(pool_setup, 3)
            for L in range(2):
                pool.memset(v_pad[L][:, :, :, HD:HD + 1], 1.0).then_inc(consts, 1)
            pool.affine_select(out=ident[:, :], in_=zeros[:, :], compare_op=ALU.not_equal, fill=1.0, base=0,
                               pattern=[[-1, P]], channel_multiplier=1).then_inc(pool_setup, 1)
            pool.wait_ge(pool_setup, 4)
            pool.tensor_copy(ident_bf[:, :], ident[:, :]).then_inc(consts, 1)
            pool.affine_select(out=mask_qk[:, :], in_=zeros[:, :], compare_op=ALU.is_ge, fill=MASKED, base=0,
                               pattern=[[-1, P]], channel_multiplier=1).then_inc(consts, 1)
            pool.affine_select(out=mask_kq[:, :], in_=zeros[:, :], compare_op=ALU.is_ge, fill=MASKED, base=0,
                               pattern=[[1, P]], channel_multiplier=-1).then_inc(consts, 1)

            pool.sem_inc(xf2_free, 1)
            pool.sem_inc(h3_free, 1)

            def alone(s, value):
                pool.wait_ge(s, value)
                pool.sem_inc(passed, 1)

            def rstd_of(n, b):
                pool.wait_ge(aggr_done[n], 2 * b + 2)
                pool.tensor_tensor(var_eps[:, n, :], mean_var[:, n, :, 1], eps[:, :], ALU.add).then_inc(eps_done[n], 1)
                pool.wait_ge(eps_done[n], b + 1)
                pool.tensor_tensor(rstd[:, n, :], var_eps[:, n, :], minus_half[:, :], ALU.pow).then_inc(rstd_done[n], 1)

            def modulate(n, b, mod_t, dst):
                pool.wait_ge(norm_done[n], 2 * b + 2)
                pool.tensor_tensor(xm[n][:, :, :], xn[n][:, :, :], bcast(mod_t[:, 1, :]), ALU.mult).then_inc(scale_done[n], 1)
                pool.wait_ge(scale_done[n], b + 1)
                pool.tensor_tensor(dst[:, :, :], xm[n][:, :, :], bcast(mod_t[:, 0, :]), ALU.add).then_inc(shift_done[n], 1)

            def low(L, b):
                pool.wait_ge(mid_done[L], b + 1)
                pool.tensor_tensor(parts[L][:, 2:6:3, :], rest[L][:, :, :], parts[L][:, 1:5:3, :],
                                   ALU.subtract).then_inc(low_done[L], 1)

            def v_half(L, b, h, i):
                if not isinstance(b, int) or b > 0:
                    pool.wait_ge(av_full, place_of(L, b - 1, 2 * h + 1) + 1)
                alone(small_free[L], bank_place(L, i, "v"))
                hs = slice(SLOTS * h, SLOTS * (h + 1))
                pool.tensor_copy(v_pad[L][:, :, hs, 0:HD],
                                 v_flat[L][:, :, :].rearrange("p t (h d) -> p t h d", d=HD)[:, :, hs, :]).then_inc(v_half_done[h][L], 1)

            def body(i):
                for turn in range(TURNS):
                    if turn == 0:
                        if live(i + 1):
                            rstd_of(0, i + 1)
                        if live(i - 1):
                            b = i - 1
                            pool.wait_ge(x_res_landed, 32 * b + 32)
                            pool.tensor_tensor(gabo[:, :], ga_bc[:, :], bo_bc[0][:, :], ALU.mult).then_inc(gabo_done, 1)
                            pool.wait_ge(gabo_done, b + 1)
                            pool.tensor_tensor(x_gabo[:, :, :], x_res[:, :, :], bcast(gabo[:, :]), ALU.add).then_inc(x_gabo_done, 1)
                        if live(i + 1):
                            pool.wait_ge(x_in_landed, 32 * (i + 2))
                            modulate(0, i + 1, mod_a, h_a)
                        if live(i):
                            v_half(0, i, 1, i - 1)
                    if turn == 1 and live(i - 1):
                        b = i - 1
                        rstd_of(1, b)
                        alone(x1_done, b + 1)
                        pool.tensor_copy(X1[:, bass.ds(b * NT, NT), :], x1[:, :, :]).then_inc(x1_kept, 1)
                        pool.wait_ge(mod_b_landed, 16 * b + 16)
                        modulate(1, b, mod_b, xf)
                    if turn == 2:
                        if live(i - 3):
                            rstd_of(3, i - 3)
                        if live(i - 1):
                            b = i - 1
                            rstd_of(2, b)
                            pool.wait_ge(shift_done[1], b + 1)
                            pool.tensor_tensor(XF[:, bass.ds(b * NT, NT), :], xf[:, :, :], bcast(bo_bc[1][:, :]),
                                               ALU.add).then_inc(xf_kept, 1)
                        if live(i - 3):
                            alone(small_free[1], bank_place(1, i, "wo"))
                            pool.tensor_copy(XF[:, bass.ds((i - 3) * NT, NT), :], xf2[:, :, :]).then_inc(xf2_free, 1)
                        if live(i - 2):
                            v_half(1, i - 2, 1, i - 1)
                    if turn == 3:
                        if live(i + 1):
                            low(0, i + 1)
                        if live(i - 3):
                            alone(small_free[1], bank_place(1, i, "h3T"))
                            pool.tensor_copy(H3[:, bass.ds((i - 3) * T, T)], h3[:, :]).then_inc(h3_free, 1)
                    if turn == 4 and live(i + 1):
                        v_half(0, i + 1, 0, i)
                    if turn == 5:
                        if live(i - 1):
                            low(1, i - 1)
                            v_half(1, i - 1, 0, i)

            over_iterations(pool, body)

            pool.wait_ge(x1_kept, B)
            for ch in range(NCH):
                tiles = slice(4 * ch, 4 * ch + 4)
                pool.wait_ge(gated, ch + 1)
                pool.tensor_tensor(X1[:, tiles, :], X1[:, tiles, :], XF[:, tiles, :], ALU.add).then_inc(final, 1)

        @block.scalar
        def _(act):
            act.wait_ge(params_in, 16 * PARAMS)
            act.activation(silu_e[:, :], c_rows[:, :], ACT.Exp, scale=-1.0).then_inc(act_setup, 1)
            act.wait_ge(pe_setup, 1)
            act.activation(qk_bias[:, :], max_bank[:, 0:4], ACT.Copy).then_inc(act_setup, 1)
            act.activation(vec[:, :], max_bank[:, 64:64 + NV + E * NJ], ACT.Copy).then_inc(act_setup, 1)
            act.activation(silu_cT[:, :], max_bank[:, 256:256 + B], ACT.Copy).then_inc(act_setup, 1)
            act.wait_ge(act_setup, 4)

            def exps(i, turn, c):
                L, b, g = group_at(i, turn)
                if not live(b):
                    return
                n = 4 * place_of(L, b, g) + c
                act.wait_ge(cols_full, n + 1)
                width = [T + P, 2 * T][L]
                p = probs[probs_of(L, b, g)][:, c, :, :].rearrange("p t q -> p (t q)")
                act.activation(p[:, 0:width], col_bank[c % 2][:, 0:width], ACT.Exp, scale=SCALE).then_inc(cols_free, 1)

            def max_to_rows(i, turn):
                L, b, g = group_at(i, turn)
                if not live(b):
                    return
                n = place_of(L, b, g)
                act.wait_ge(maxT_full, n + 1)
                at_least(act, shift_landed, 16 * n)
                act.activation(max_rows[:, :], max_rows_ps[0:2 * GH, 0:T], ACT.Copy).then_inc(maxT_free, 1)

            def shift_rows(i, turn):
                L, b, g = group_at(i, turn)
                if not live(b):
                    return
                h, s = g // 2, GH * (g % 2)
                act.wait_ge(maxT_free, place_of(L, b, g) + 1)
                dst = stacked[L][64 * h + QROWS:64 * h + SROWS, s:s + GH, 0, :]
                act.dma_start(dst, max_rows[:, :]).then_inc(shift_landed, 16)

            def y_out(i, turn):
                L, b, g = group_at(i, turn)
                if not live(b):
                    return
                n = place_of(L, b, g)
                act.wait_ge(av_full, n + 1)
                act.activation(y_sb[L][:, :], av_bank[:, 0:T], ACT.Copy).then_inc(y_sb_done, 1)

            def hT_out(L, b, i):
                act.wait_ge(small_full[L], bank_place(L, i, "xT"))
                if L == 0:
                    act.activation(hT[0][:, :], small[0][:, 0:T], ACT.Copy).then_inc(small_free[0], 1)
                else:
                    act.activation(hT[1][:, :], small[1][:, 0:T], ACT.Identity, bias=vec[:, B1_:B1_ + 1],
                                   scale=vec[:, G1:G1 + 1]).then_inc(small_free[1], 1)

            def high(L, b, i):
                act.wait_ge(small_full[L], bank_place(L, i, "qk"))
                at_least(act, half_landed[1][L], 16 * (6 * b + 1))
                for n in range(2):
                    act.activation(parts[L][:, 3 * n, :], small[L][:, T * n:T * (n + 1)], ACT.Identity,
                                   bias=qk_bias[:, 2 * L + n:2 * L + n + 1]).then_inc(high_done[L], 1)

            def mid(L, b, i):
                act.wait_ge(small_free[L], bank_place(L, i, "qk"))
                act.activation(parts[L][:, 1:5:3, :], rest[L][:, :, :], ACT.Copy).then_inc(mid_done[L], 1)

            def v_out(L, b, i):
                act.wait_ge(small_full[L], bank_place(L, i, "v"))
                at_least(act, v_half_done[1][L], b)
                act.activation(v_flat[L][:, :, :].rearrange("p t c -> p (t c)"), small[L][:, 0:T], ACT.Copy).then_inc(small_free[L], 1)

            def yT_out(L, b, i):
                act.wait_ge(small_full[L], bank_place(L, i, "y2T"))
                act.activation(yT[L][:, :], small[L][:, 0:T], ACT.Identity,
                               bias=vec[:, BV0 + L:BV0 + L + 1]).then_inc(small_free[L], 1)

            def body(i):
                for turn in range(TURNS):
                    for c in range(GH):
                        exps(i, turn, c)
                        if c == 1:
                            max_to_rows(i, turn + 2)
                        if c == 2:
                            shift_rows(i, turn + 2)
                            y_out(i, turn - 1)
                        at = (turn, c)
                        if at == (0, 3) and live(i - 1):
                            yT_out(0, i - 1, i)
                        if at == (1, 3) and live(i + 1):
                            hT_out(0, i + 1, i)
                        if at == (1, 3) and live(i - 3):
                            yT_out(1, i - 3, i)
                        if at == (2, 1) and live(i + 1):
                            high(0, i + 1, i)
                        if at == (3, 0) and live(i + 1):
                            mid(0, i + 1, i)
                        if at == (2, 3) and live(i + 1):
                            v_out(0, i + 1, i)
                        if at == (3, 2) and live(i - 3):
                            act.wait_ge(small_full[1], bank_place(1, i, "h3T"))
                            at_least(act, h3_free, i - 2)
                            act.activation(h3[:, :], small[1][:, 0:T], ACT.Identity, bias=vec[:, B2_:B2_ + 1],
                                           scale=vec[:, G2:G2 + 1]).then_inc(small_free[1], 1)
                        if at == (3, 3) and live(i - 1):
                            hT_out(1, i - 1, i)
                        if at == (4, 1) and live(i - 1):
                            high(1, i - 1, i)
                        if at == (4, 3) and live(i - 1):
                            mid(1, i - 1, i)
                        if at == (5, 0) and live(i - 1):
                            v_out(1, i - 1, i)

            over_iterations(act, body)

            act.wait_ge(top_step, TOP_DIF)
            act.activation(t_exp[:, :, :], t_dif[:, :, :], ACT.Exp).then_inc(ew_exp, 1)
            for q in range(TILES // 4):
                act.wait_ge(ewT_full, q + 1)
                act.activation(ewT[:, 512 * q:512 * q + 512], bank[q][0:E, :], ACT.Copy).then_inc(ewT_done, 1)
            def relus(m):
                for n in range(2):
                    e = m * 2 + n
                    for ch in range(NCH):
                        for j in range(NJ):
                            act.wait_ge(up_full, (e * NCH + ch) * NJ + j + 1)
                            if ch == 0 and j == 0:
                                act.wait_ge(cols_e, 2 * e + 2)
                            act.activation(hid[ch % 2][:, j, :], bank[j][:, :], ACT.Relu,
                                           bias=b1_e[n][:, j:j + 1]).then_inc(relu_done, 1)

            over_experts(act, relus)

        @block.vector
        def _(dve):
            dve.wait_ge(params_in, 16 * PARAMS)
            steps = [0]

            def link(ins):
                steps[0] += 1
                ins.then_inc(dve_setup, 1)
                dve.wait_ge(dve_setup, steps[0])

            def permuted(dst, src):
                return (dst.rearrange("p (a d s) -> p a s d", a=2, d=HD), src.rearrange("p (a s d) -> p a s d", a=2, s=SLOTS))
            for L in range(2):
                for n in range(2):
                    for a in range(2):
                        o, s = permuted(w_qk[L][:, n, :], w_in[L][:, C * n:C * (n + 1)])
                        dve.tensor_copy(o[:, a], s[:, a])
            for a in range(2):
                o, s = permuted(qk_rows_p[:, :], qk_rows[:, :])
                ins = dve.tensor_copy(o[:, a], s[:, a])
            link(ins)
            dve.wait_ge(act_setup, 1)
            link(dve.tensor_scalar(silu_r[:, :], silu_e[:, :], 1.0, None, ALU.add))
            link(dve.reciprocal(silu_e[:, :], silu_r[:, :]))
            link(dve.tensor_tensor(silu_c[:, :], c_rows[:, :], silu_e[:, :], ALU.mult))
            assert steps[0] == SETUP_SILU
            dve.wait_ge(pe_setup, 2)
            m2 = mod[:, :, :].rearrange("b m c -> b (m c)")
            dve.tensor_copy(m2[:, 0:512], bank[0][0:B, :])
            link(dve.tensor_copy(m2[:, 512:768], bank[1][0:B, 0:256]))
            for m in (CA, CB):
                link(dve.tensor_scalar(mod[:, m, :], mod[:, m, :], 1.0, None, ALU.add))
            gates = mod[:, GA:GB + 1:GB - GA, :]
            link(dve.tensor_scalar(mod_sign[:, :, :], gates, 0.0, 2.0, ALU.is_ge, ALU.mult))
            link(dve.tensor_scalar(mod_sign[:, :, :], mod_sign[:, :, :], -1.0, None, ALU.add))
            link(dve.scalar_tensor_tensor(out=mod_abs[:, :, :], in0=gates, scalar=-1.0, in1=gates, op0=ALU.mult, op1=ALU.max))
            link(dve.scalar_tensor_tensor(out=gates, in0=mod_abs[:, :, :], scalar=0.25, in1=mod_sign[:, :, :],
                                          op0=ALU.max, op1=ALU.mult))
            assert steps[0] == SETUP_MOD

            def alone(s, value):
                dve.wait_ge(s, value)
                dve.sem_inc(passed, 1)

            def norm_stats(n, b, src):
                for t in range(NT):
                    dve.bn_stats(stats[:, n, t, :], src[:, t, :]).then_inc(stats_done[n], 1)
                alone(stats_done[n], 2 * b + 2)
                for t in range(NT):
                    dve.bn_aggr(mean_var[:, n, t, :], stats[:, n, t, :]).then_inc(aggr_done[n], 1)

            def normalize(n, b, src):
                dve.wait_ge(rstd_done[n], b + 1)
                dve.wait_ge(aggr_done[n], 2 * b + 2)
                for t in range(NT):
                    dve.tensor_scalar(xn[n][:, t, :], src[:, t, :], mean_var[:, n, t, 0:1], rstd[:, n, t:t + 1],
                                      ALU.subtract, ALU.mult).then_inc(norm_done[n], 1)

            def row_max(i, turn, c):
                L, b, g = group_at(i, turn)
                if not live(b):
                    return
                n = 4 * place_of(L, b, g) + c
                dve.wait_ge(rows_full, n + 1)
                if c == 0:
                    at_least(dve, max_split[L], 2 * (4 * b + g))
                blocks, width = [(3, P), (2, T)][L]
                src = row_bank[c % 2][:, 0:blocks * width].rearrange("p (a k) -> p a k", a=blocks)
                dve.tensor_reduce(neg_max[L][:, :, c], src, AX.X, ALU.max, negate=True).then_inc(rows_free, 1)

            def split_max(i, turn):
                L, b, g = group_at(i, turn)
                if not live(b):
                    return
                n = 4 * b + g
                dve.wait_ge(rows_free, 4 * place_of(L, b, g) + 4)
                if L == 0:
                    dve.tensor_tensor(neg_max[0][:, 1, :], neg_max[0][:, 1, :], neg_max[0][:, 2, :],
                                      ALU.min).then_inc(max_step[0], 1)
                    dve.wait_ge(max_step[0], n + 1)
                if not isinstance(b, int) or n > 0:
                    pb_, pg = (b, g - 1) if g > 0 else (b - 1, GROUPS - 1)
                    dve.wait_ge(maxT_full, place_of(L, pb_, pg) + 1)
                dve.tensor_copy(max_parts[L][:, :, 0, :], neg_max[L][:, 0:2, :]).then_inc(max_split[L], 1)
                dve.wait_ge(max_split[L], 2 * n + 1)
                dve.tensor_tensor(max_parts[L][:, :, 1, :], neg_max[L][:, 0:2, :], max_parts[L][:, :, 0, :],
                                  ALU.subtract).then_inc(max_split[L], 1)

            def y_normalize(i, turn):
                L, b, g = group_at(i, turn)
                if not live(b):
                    return
                n = 4 * b + g
                dve.wait_ge(small_full[L], bank_place(L, i, "yT", g))
                ps = small[L][:, 0:T].rearrange("p (t c w) -> p t c w", t=NT, c=GH)
                dve.reciprocal(y_inv[L][:, :, :, :], ps[:, :, :, HD:HD + 1]).then_inc(inv_done[L], 1)
                dve.wait_ge(inv_done[L], n + 1)
                ins = None
                for t in range(NT):
                    ins = dve.tensor_tensor(y_norm[L][:, t, GH * g:GH * g + GH, :], ps[:, t, :, 0:HD],
                                            y_inv[L][:, t, :, :].to_broadcast([P, GH, HD]), ALU.mult)
                    if t == NT - 1:
                        ins.then_inc(small_free[L], 1)

            def rest_of(L, b, i):
                dve.wait_ge(high_done[L], 2 * b + 2)
                at_least(dve, low_done[L], b)
                for n in range(2):
                    ins = dve.scalar_tensor_tensor(out=rest[L][:, n, :], in0=small[L][:, T * n:T * (n + 1)],
                                                   scalar=qk_bias[:, 2 * L + n:2 * L + n + 1], in1=parts[L][:, 3 * n, :],
                                                   op0=ALU.add, op1=ALU.subtract)
                ins.then_inc(small_free[L], 1)

            def body(i):
                for turn in range(TURNS):
                    for c in range(GH):
                        row_max(i, turn + 3, c)
                        at = (turn, c)
                        if c == 1:
                            y_normalize(i, turn - 2)
                        if at == (0, 0) and live(i + 1):
                            dve.wait_ge(x_in_landed, 32 * (i + 2))
                            norm_stats(0, i + 1, x_in)
                        if at == (0, 1) and live(i + 1):
                            at_least(dve, scale_done[0], i + 1)
                            normalize(0, i + 1, x_in)
                        if at == (1, 1) and live(i - 1):
                            b = i - 1
                            dve.wait_ge(small_full[0], bank_place(0, i, "wo"))
                            dve.wait_ge(x_res_landed, 32 * b + 32)
                            dve.tensor_tensor(attn_g[:, :, :], small[0][:, 0:T].rearrange("p (t c) -> p t c", t=NT),
                                              bcast(ga_bc[:, :]), ALU.mult).then_inc(small_free[0], 1)
                            dve.wait_ge(small_free[0], bank_place(0, i, "wo"))
                            dve.wait_ge(x_gabo_done, b + 1)
                            at_least(dve, x1_kept, b)
                            dve.tensor_tensor(x1[:, :, :], attn_g[:, :, :], x_gabo[:, :, :], ALU.add).then_inc(x1_done, 1)
                            dve.wait_ge(x1_done, b + 1)
                            norm_stats(1, b, x1)
                        if at == (1, 2) and live(i - 1):
                            at_least(dve, scale_done[1], i - 1)
                            normalize(1, i - 1, x1)
                        if at == (2, 1) and live(i - 3):
                            b = i - 3
                            dve.wait_ge(small_full[1], bank_place(1, i, "wo"))
                            dve.wait_ge(xf_kept, b + 1)
                            dve.wait_ge(xf2_free, b + 1)
                            dve.tensor_tensor(xf2[:, :, :], XF[:, bass.ds(b * NT, NT), :],
                                              small[1][:, 0:T].rearrange("p (t c) -> p t c", t=NT), ALU.add).then_inc(small_free[1], 1)
                            dve.wait_ge(small_free[1], bank_place(1, i, "wo"))
                            norm_stats(3, b, xf2)
                        if at == (2, 2) and live(i + 1):
                            rest_of(0, i + 1, i)
                        if at == (2, 1) and live(i - 1):
                            dve.wait_ge(shift_done[1], i)
                            norm_stats(2, i - 1, xf)
                        if at == (2, 2) and live(i - 3):
                            normalize(3, i - 3, xf2)
                        if at == (2, 3) and live(i - 1):
                            normalize(2, i - 1, xf)
                        if at == (4, 0) and live(i - 3):
                            b = i - 3
                            dve.wait_ge(small_full[1], bank_place(1, i, "gate"))
                            dve.tensor_tensor(LG[:, bass.ds(b * NT, NT), :],
                                              small[1][:, 0:NT * E].rearrange("p (t e) -> p t e", t=NT),
                                              gate_b[:, None, :].to_broadcast([P, NT, E]), ALU.add).then_inc(small_free[1], 1)
                        if at == (4, 2) and live(i - 1):
                            rest_of(1, i - 1, i)
                    split_max(i, turn + 3)

            over_iterations(dve, body)

            made = [0]

            def then(ins):
                made[0] += 1
                ins.then_inc(top_step, 1)
                dve.wait_ge(top_step, made[0])
            dve.wait_ge(consts, CONSTS)
            dve.wait_ge(small_free[1], bank_place(1, B + 2, "gate"))
            for t in range(TILES):
                ins = dve.max(top[:, t, :], LG[:, t, :])
            then(ins)
            for t in range(TILES):
                dve.max_index(top_i[:, t, :], top[:, t, :], LG[:, t, :])
            ins = dve.tensor_tensor(t_dif[:, :, :], top[:, :, 1:2], top[:, :, 0:1], ALU.subtract)
            then(ins)
            assert made[0] == TOP_DIF
            then(dve.tensor_copy(top_f[:, :, :], top_i[:, :, 0:2]))
            dve.wait_ge(ew_exp, 1)
            then(dve.tensor_scalar(t_sum[:, :, :], t_exp[:, :, :], 1.0, None, ALU.add))
            then(dve.reciprocal(w_top[:, 0, :, :], t_sum[:, :, :]))
            then(dve.tensor_tensor(w_top[:, 1, :, :], w_top[:, 0, :, :], t_exp[:, :, :], ALU.mult))
            iotas = iota_e[:, None, :].to_broadcast([P, TILES, E])
            for k in range(2):
                then(dve.tensor_tensor(pick[:, k, :, :], iotas, top_f[:, :, k:k + 1].to_broadcast([P, TILES, E]), ALU.is_equal))
                then(dve.tensor_tensor(pick[:, k, :, :], pick[:, k, :, :], w_top[:, k, :, :].to_broadcast([P, TILES, E]), ALU.mult))
            then(dve.tensor_tensor(EW[:, :, :], pick[:, 0, :, :], pick[:, 1, :, :], ALU.add))
            assert made[0] == TOP_ALL
            dve.wait_ge(xf2_free, B + 1)
            for ch in range(NCH):
                dve.wait_ge(b2_full, ch + 1)
                tiles = slice(4 * ch, 4 * ch + 4)
                dve.tensor_tensor(XF[:, tiles, :], XF[:, tiles, :],
                                  bank[4 + ch % 2][:, :].rearrange("p (t c) -> p t c", t=4), ALU.add).then_inc(b2_added, 1)
            dve.wait_ge(b2_added, NCH)

            def accumulate(m):
                for n in range(2):
                    e = m * 2 + n
                    dve.tensor_copy(ew_e[n][:, :], EW[:, :, bass.ds(e, 1)].rearrange("p t o -> p (t o)")).then_inc(cols_e, 1)
                    dve.tensor_copy(b1_e[n][:, :], vec[:, bass.ds(e * NJ + NV, NJ)]).then_inc(cols_e, 1)
                    dve.wait_ge(cols_e, 2 * e + 2)
                    for ch in range(NCH):
                        dve.wait_ge(down_full, e * NCH + ch + 1)
                        at_least(dve, acc_done, (e - 1) * NCH + ch + 1)
                        for k in range(4):
                            t = 4 * ch + k
                            ins = dve.scalar_tensor_tensor(out=XF[:, t, :], in0=bank[4 + ch % 2][:, P * k:P * (k + 1)],
                                                           scalar=ew_e[n][:, t:t + 1], in1=XF[:, t, :],
                                                           op0=ALU.mult, op1=ALU.add)
                        ins.then_inc(acc_done, 1)
            over_experts(dve, accumulate)
            dve.wait_ge(acc_done, E * NCH)
            dve.wait_ge(gb_landed, 16 * B)
            for ch in range(NCH):
                f = XF[:, 4 * ch:4 * ch + 4, :].rearrange("p (b t) c -> p b t c", t=NT)
                g = GBC[:, 2 * ch:2 * ch + 2, None, :].to_broadcast([P, 2, NT, C])
                dve.tensor_tensor(f, f, g, ALU.mult).then_inc(gated, 1)

        @block.tensor
        def _(pe):
            pe.wait_ge(consts, CONSTS)
            pe.wait_ge(dve_setup, SETUP_SILU)
            pe.transpose(max_bank[:, 0:4], qk_rows_p[:, :], ident[0:4, 0:4])
            nv = NV + E * NJ
            pe.transpose(max_bank[:, 64:64 + nv], vec_rows[:, :], ident[0:nv, 0:nv])
            pe.transpose(max_bank[:, 256:256 + B], silu_c[:, :], ident[0:B, 0:B]).then_inc(pe_setup, 1)
            pe.wait_ge(act_setup, 4)
            pe.matmul(bank[0][0:B, :], silu_cT[:, :], wmod[:, 0:512], start=True, stop=True)
            pe.matmul(bank[1][0:B, 0:256], silu_cT[:, :], wmod[:, 512:768], start=True, stop=True).then_inc(pe_setup, 1)
            pe.wait_ge(dve_setup, SETUP_SILU + 1)

            def scores_rows(i, turn, c):
                L, b, g = group_at(i, turn)
                if not live(b):
                    return
                n = 4 * place_of(L, b, g) + c
                h, s = g // 2, GH * (g % 2) + c
                if c == 0 and g % 2 == 0:
                    pe.wait_ge(half_landed[h][L], 16 * (1 + 6 * (b + 1)))
                at_least(pe, rows_free, n - 1)
                q = stacked[L][half_rows[h], s, 0, :]
                k = stacked[L][half_rows[h], s, 1, :]
                ps = row_bank[c % 2]
                pos = (64 * h, 0)
                if L == 0:
                    pe.matmul(ps[:, 0:P], q[:, 0:P], k[:, 0:P], start=True, stop=True, tile_position=pos)
                    pe.matmul(ps[:, 0:P], ident_bf[:, :], mask_qk[:, :], start=False, stop=True, skip_group_check=True)
                    pe.matmul(ps[:, P:3 * P], q[:, P:T], k[:, :], start=True, stop=True, tile_position=pos)
                    ins = pe.matmul(ps[:, 2 * P:3 * P], ident_bf[:, :], mask_qk[:, :], start=False, stop=True,
                                    skip_group_check=True)
                else:
                    pe.matmul(ps[:, 0:T], q[:, 0:P], k[:, :], start=True, stop=True, tile_position=pos)
                    ins = pe.matmul(ps[:, T:2 * T], q[:, P:T], k[:, :], start=True, stop=True, tile_position=pos)
                ins.then_inc(rows_full, 1)

            def scores_cols(i, turn, c):
                L, b, g = group_at(i, turn)
                if not live(b):
                    return
                n = 4 * place_of(L, b, g) + c
                h, s = g // 2, GH * (g % 2) + c
                if c == 0:
                    pe.wait_ge(shift_landed, 16 * (place_of(L, b, g) + 1))
                at_least(pe, cols_free, n - 1)
                q = stacked[L][64 * h:64 * h + SROWS, s, 0, :]
                k = stacked[L][64 * h:64 * h + SROWS, s, 1, :]
                ps = col_bank[c % 2]
                pos = (64 * h, 0)
                if L == 0:
                    pe.matmul(ps[:, 0:T], k[:, 0:P], q[:, :], start=True, stop=True, tile_position=pos)
                    pe.matmul(ps[:, 0:P], ident_bf[:, :], mask_kq[:, :], start=False, stop=True, skip_group_check=True)
                    pe.matmul(ps[:, T:T + P], k[:, P:T], q[:, P:T], start=True, stop=True, tile_position=pos)
                    ins = pe.matmul(ps[:, T:T + P], ident_bf[:, :], mask_kq[:, :], start=False, stop=True, skip_group_check=True)
                else:
                    pe.matmul(ps[:, 0:T], k[:, 0:P], q[:, :], start=True, stop=True, tile_position=pos)
                    ins = pe.matmul(ps[:, T:2 * T], k[:, P:T], q[:, :], start=True, stop=True, tile_position=pos)
                ins.then_inc(cols_full, 1)

            def max_transposes(i, turn):
                L, b, g = group_at(i, turn)
                if not live(b):
                    return
                n = place_of(L, b, g)
                pe.wait_ge(max_split[L], 2 * (4 * b + g) + 2)
                at_least(pe, maxT_free, n)
                for t in range(NT):
                    ins = pe.transpose(max_rows_ps[0:2 * GH, P * t:P * (t + 1)],
                                       max_parts[L][:, t, :, :].rearrange("p a c -> p (a c)"), ident_bf[:, :])
                ins.then_inc(maxT_full, 1)

            def weighted_values(i, turn):
                L, b, g = group_at(i, turn)
                if not live(b):
                    return
                n = place_of(L, b, g)
                pe.wait_ge(cols_free, 4 * n + 4)
                if g % 2 == 0:
                    pe.wait_ge(v_half_done[g // 2][L], b + 1)
                at_least(pe, y_sb_done, n)
                p = probs[probs_of(L, b, g)]
                for t in range(NT):
                    for c in range(GH):
                        ps = av_bank[VW * c:VW * (c + 1), 0:T]
                        v = v_pad[L][:, t, GH * g + c, :]
                        pc = p[:, c, :, :].rearrange("p t q -> p (t q)")
                        if L == 0 and t == 1:
                            ins = pe.matmul(ps[:, P:T], v, pc[:, T:T + P], start=False, stop=True,
                                            tile_position=(0, VW * c), skip_group_check=True)
                        else:
                            ins = pe.matmul(ps, v, pc[:, T * t:T * (t + 1)], start=(t == 0), stop=(t == 1),
                                            tile_position=(0, VW * c), skip_group_check=True)
                ins.then_inc(av_full, 1)

            def fill(L, place):
                if isinstance(place, int):
                    at_least(pe, small_free[L], place - 1)
                else:
                    pe.wait_ge(small_free[L], place - 1)

            def y_transposes(i, turn):
                L, b, g = group_at(i, turn)
                if not live(b):
                    return
                fill(L, bank_place(L, i, "yT", g))
                pe.wait_ge(y_sb_done, place_of(L, b, g) + 1)
                for t in range(NT):
                    ins = pe.transpose(small[L][:, P * t:P * (t + 1)], y_sb[L][:, P * t:P * (t + 1)], ident[:, :])
                ins.then_inc(small_full[L], 1)

            def tiles_T(L, i, what, src):
                for t in range(NT):
                    ins = pe.transpose(small[L][:, P * t:P * (t + 1)], src[:, t, :], ident[:, :])
                ins.then_inc(small_full[L], 1)

            def project_y(L, i, b):
                fill(L, bank_place(L, i, "wo"))
                for t in range(NT):
                    ins = pe.matmul(small[L][:, C * t:C * (t + 1)], yT[L][:, P * t:P * (t + 1)], w_out[L][:, :],
                                    start=True, stop=True)
                ins.then_inc(small_full[L], 1)

            def project_qk(L, i, b):
                fill(L, bank_place(L, i, "qk"))
                for n in range(2):
                    ins = pe.matmul(small[L][:, T * n:T * (n + 1)], w_qk[L][:, n, :], hT[L][:, :], start=True, stop=True)
                ins.then_inc(small_full[L], 1)

            def project_v(L, i, b):
                fill(L, bank_place(L, i, "v"))
                for t in range(NT):
                    ins = pe.matmul(small[L][:, C * t:C * (t + 1)], hT[L][:, P * t:P * (t + 1)],
                                    w_in[L][:, 2 * C:3 * C], start=True, stop=True)
                ins.then_inc(small_full[L], 1)

            def y2T(L, i, b):
                place = bank_place(L, i, "y2T")
                fill(L, place)
                tiles_T(L, i, "y2T", y_norm[L][:, :, :, :].rearrange("p t h d -> p t (h d)"))

            def body(i):
                for turn in range(TURNS):
                    for c in range(GH):
                        scores_cols(i, turn, c)
                        scores_rows(i, turn + 3, c)
                        at = (turn, c)
                        if c == 0:
                            y_transposes(i, turn - 2)
                            max_transposes(i, turn + 2)
                        if c == 1:
                            weighted_values(i, turn - 1)
                        if at == (0, 2) and live(i - 1):
                            y2T(0, i, i - 1)
                        if at == (1, 0) and live(i - 1):
                            project_y(0, i, i - 1)
                        if at == (1, 2) and live(i + 1):
                            fill(0, bank_place(0, i, "xT"))
                            pe.wait_ge(shift_done[0], i + 2)
                            tiles_T(0, i, "xT", h_a)
                        if at == (1, 2) and live(i - 3):
                            y2T(1, i, i - 3)
                        if at == (2, 0) and live(i - 3):
                            project_y(1, i, i - 3)
                        if at == (2, 1) and live(i + 1):
                            project_qk(0, i, i + 1)
                        if at == (2, 3) and live(i + 1):
                            project_v(0, i, i + 1)
                        if at == (3, 1) and live(i - 3):
                            fill(1, bank_place(1, i, "h3T"))
                            pe.wait_ge(norm_done[3], 2 * (i - 3) + 2)
                            tiles_T(1, i, "h3T", xn[3])
                        if at == (3, 2) and live(i - 1):
                            fill(1, bank_place(1, i, "xT"))
                            pe.wait_ge(norm_done[2], 2 * (i - 1) + 2)
                            tiles_T(1, i, "xT", xn[2])
                        if at == (3, 3) and live(i - 3):
                            fill(1, bank_place(1, i, "gate"))
                            for t in range(NT):
                                ins = pe.matmul(small[1][:, E * t:E * (t + 1)], h3[:, P * t:P * (t + 1)], gate_w[:, :],
                                                start=True, stop=True)
                            ins.then_inc(small_full[1], 1)
                        if at == (4, 0) and live(i - 1):
                            project_qk(1, i, i - 1)
                        if at == (4, 3) and live(i - 1):
                            project_v(1, i, i - 1)

            over_iterations(pe, body)

            pe.wait_ge(top_step, TOP_ALL)
            for q in range(TILES // 4):
                for k in range(4):
                    ins = pe.transpose(bank[q][0:E, P * k:P * (k + 1)], EW[:, 4 * q + k, :], ident[:, :])
                ins.then_inc(ewT_full, 1)
            pe.wait_ge(ewT_done, TILES // 4)
            for ch in range(NCH):
                at_least(pe, b2_added, ch - 1)
                for k in range(4):
                    t = 4 * ch + k
                    ins = pe.matmul(bank[4 + ch % 2][:, P * k:P * (k + 1)], ewT[:, P * t:P * (t + 1)], b2_rows[:, :],
                                    start=True, stop=True)
                ins.then_inc(b2_full, 1)
            pe.wait_ge(b2_added, NCH)
            pe.wait_ge(h3_free, B + 1)

            def experts(m):
                for n in range(2):
                    e = m * 2 + n
                    pe.wait_ge(w_landed[n], m * 32 + 32)
                    for ch in range(NCH):
                        for j in range(NJ):
                            at_least(pe, relu_done, (e * NCH + ch - 1) * NJ + j + 1)
                            pe.matmul(bank[j][:, :], W1[n][:, P * j:P * (j + 1)], H3[:, 512 * ch:512 * (ch + 1)],
                                      start=True, stop=True).then_inc(up_full, 1)
                        at_least(pe, acc_done, e * NCH + ch - 1)
                        pe.wait_ge(relu_done, (e * NCH + ch + 1) * NJ)
                        for k in range(4):
                            for j in range(NJ):
                                ins = pe.matmul(bank[4 + ch % 2][:, P * k:P * (k + 1)], hid[ch % 2][:, j, P * k:P * (k + 1)],
                                                W2[n][:, j, :], start=(j == 0), stop=(j == NJ - 1))
                        ins.then_inc(down_full, 1)

            over_experts(pe, experts)


_INS = ['L0_attn_x', 'L0_attn_Wq', 'L0_attn_bq', 'L0_attn_Wk', 'L0_attn_bk', 'L0_attn_Wv', 'L0_attn_bv',
        'L0_attn_Wo', 'L0_attn_bo', 'L0_ffn_ln1_g', 'L0_ffn_ln1_b', 'L0_ffn_w_qkv', 'L0_ffn_b_qkv', 'L0_ffn_w_o',
        'L0_ffn_b_o', 'L0_ffn_ln2_g', 'L0_ffn_ln2_b', 'L0_ffn_gate_w', 'L0_ffn_gate_b', 'L0_ffn_W1', 'L0_ffn_b1',
        'L0_ffn_W2', 'L0_ffn_b2', 'L0_c', 'L0_wmod']


def kernel(**inputs):
    import numpy as _np
    import concourse.bacc as _bacc
    from concourse import mybir as _mybir
    from concourse.bass_utils import run_bass_kernel_spmd as _run

    nc = _bacc.Bacc("TRN2", target_bir_lowering=False, num_devices=1)
    arrays, io = {}, {}
    for name in _INS:
        a = _np.ascontiguousarray(inputs[name])
        arrays[f"in_{name}"] = a
        io[name] = nc.dram_tensor(f"in_{name}", a.shape, _mybir.dt.from_np(a.dtype), kind="ExternalInput").ap()
    batches = inputs["L0_c"].shape[0]
    out = nc.dram_tensor("out_0", inputs["L0_attn_x"].shape, _mybir.dt.float32, kind="ExternalOutput").ap()
    mod_dram = nc.dram_tensor("mod_rows", (batches, inputs["L0_wmod"].shape[1]), _mybir.dt.float32, kind="Internal").ap()
    build(nc, io, out, mod_dram)
    r = _run(nc, [arrays], core_ids=[0])
    return r.results[0]["out_0"]
```

```python
from contextlib import ExitStack

import concourse.bass as bass
from concourse import mybir

F32 = mybir.dt.float32
BF16 = mybir.dt.bfloat16
F32R = mybir.dt.float32r
U32 = mybir.dt.uint32
ALU = mybir.AluOpType
ACT = mybir.ActivationFunctionType
AX = mybir.AxisListType

P = 128
HD = 8
HEADS = 16
GH = 4
GROUPS = HEADS // GH
SLOTS = HEADS // 2
QROWS = 6 * HD
SROWS = QROWS + 2
VW = 32
TURNS = 2 * GROUPS
EPS = 1e-5
SCALE = HD ** -0.5
MASKED = -1e30
TOPK_W = 8
PAIRS = [(0, 0), (0, 1), (0, 2), (1, 0), (1, 1), (2, 0)]
SA, CA, GA, SB_, CB, GB = range(6)
PARAMS = 23
CONSTS = 9
SETUP_SILU, SETUP_MOD = 4, 11
TOP_DIF, TOP_ALL = 2, 11


def at_least(eng, sem, value):
    if isinstance(value, int) and value <= 0:
        return
    eng.wait_ge(sem, value)


def build(nc, io, out, mod_dram, ew_dram):
    x_dram = io["L0_attn_x"]
    B, T, C = x_dram.shape
    E = io["L0_ffn_gate_w"].shape[1]
    DFF = io["L0_ffn_W1"].shape[2]
    NJ = DFF // P
    NT = T // P
    TILES = B * NT
    LAG = 2 * GROUPS + 1
    LOOP = (3, B - 1)
    assert C == P and NT == 2 and T == 256

    def live(b):
        return not isinstance(b, int) or 0 <= b < B

    def is_first(i, n):
        return isinstance(i, int) and i == n

    def group_at(i, turn):
        if turn < 0:
            i, turn = i - 1, turn + TURNS
        if turn >= TURNS:
            i, turn = i + 1, turn - TURNS
        k = turn // 2
        if turn % 2 == 0:
            return 0, i, k
        return (1, i - 3, GROUPS - 1) if k == 0 else (1, i - 2, k - 1)

    def place_of(L, b, g):
        n = GROUPS * b + g
        if L == 0:
            return n if isinstance(b, int) and n < LAG else 2 * n - LAG
        return 2 * n + LAG + 1 if not isinstance(b, int) or n < GROUPS * B - LAG else n + GROUPS * B

    def probs_of(L, b, g):
        n = place_of(L, b, g)
        return n % 2 if isinstance(n, int) else (1 - L if LAG % 2 else L)

    def bank_uses(L, i):
        if L == 0:
            order = [("yT", i - 1, 3), ("y2T", i - 1, 0), ("wo", i - 1, 0), ("xT", i + 1, 0), ("yT", i, 0),
                     ("qk", i + 1, 0), ("v", i + 1, 0), ("yT", i, 1), ("yT", i, 2)]
        else:
            order = [("yT", i - 3, 2), ("yT", i - 3, 3), ("xT", i - 1, 0), ("qk", i - 1, 0), ("y2T", i - 3, 0),
                     ("yT", i - 2, 0), ("v", i - 1, 0), ("wo", i - 3, 0), ("h3T", i - 3, 0), ("yT", i - 2, 1),
                     ("gate", i - 3, 0)]
        return [u for u in order if live(u[1])]

    def bank_place(L, i, what, g=0):
        n = i if isinstance(i, int) else LOOP[0]
        before = sum(len(bank_uses(L, m)) for m in range(-1, n))
        names = [(u[0], u[2]) for u in bank_uses(L, n)]
        here = before + names.index((what, g)) + 1
        if isinstance(i, int):
            return here
        return (i - LOOP[0]) * len(bank_uses(L, n)) + here

    ctx = ExitStack()
    with ctx:
        def sb(name, shape, dt=F32):
            return ctx.enter_context(nc.sbuf_tensor(name, shape, dt))

        def pb(name, shape, dt=F32):
            return ctx.enter_context(nc.psum_tensor(name, shape, dt))

        def sem(name):
            return ctx.enter_context(nc.semaphore(name))

        def sems(name):
            return [sem(f"{name}{L}") for L in range(2)]

        w_in = [sb("w_in0", [P, 3 * C]), sb("w_in1", [P, 3 * C])]
        w_qk = [sb(f"w_qk{L}", [P, 2, C]) for L in range(2)]
        w_out = [sb("w_out0", [P, C]), sb("w_out1", [P, C])]
        gate_w = sb("gate_w", [P, E])
        wmod = sb("wmod", [P, 6 * C])
        c_rows = sb("c_rows", [B, C])
        qk_rows = sb("qk_rows", [4, C])
        qk_rows_p = sb("qk_rows_p", [4, C])
        NV = 6
        vec_rows = sb("vec_rows", [NV + E * NJ, C])
        qk_bias = sb("qk_bias", [P, 4])
        vec = sb("vec", [P, NV + E * NJ])
        BV0, BV1, G1, B1_, G2, B2_ = range(NV)
        b2_rows = sb("b2_rows", [E, C])
        gate_b = sb("gate_b", [P, E])
        bo_bc = [sb("bo_bc0", [P, C]), sb("bo_bc1", [P, C])]
        ident = sb("ident", [P, P])
        ident_bf = sb("ident_bf", [P, P], BF16)
        zeros = sb("zeros", [P, P])
        mask_qk = sb("mask_qk", [P, P], BF16)
        mask_kq = sb("mask_kq", [P, P], BF16)
        eps = sb("eps", [P, NT])
        minus_half = sb("minus_half", [P, NT])
        silu_e = sb("silu_e", [B, C])
        silu_r = sb("silu_r", [B, C])
        silu_c = sb("silu_c", [B, C])
        silu_cT = sb("silu_cT", [P, B])
        mod = sb("mod", [B, 6, C])
        mod_sign = sb("mod_sign", [B, 2, C])
        mod_abs = sb("mod_abs", [B, 2, C])

        gabo = sb("gabo", [P, C])
        x_gabo = sb("x_gabo", [P, NT, C])
        attn_g = sb("attn_g", [P, NT, C])
        xf = sb("xf", [P, NT, C])
        stats = sb("stats", [P, 4, NT, 6])
        mean_var = sb("mean_var", [P, 4, NT, 2])
        var_eps = sb("var_eps", [P, 4, NT])
        rstd = sb("rstd", [P, 4, NT])
        xn = [sb(f"xn{n}", [P, NT, C]) for n in range(4)]
        xm = [sb(f"xm{n}", [P, NT, C]) for n in range(2)]
        h_a = sb("h_a", [P, NT, C])
        hT = [sb(f"hT{L}", [P, T]) for L in range(2)]
        parts = [sb(f"parts{L}", [P, 6, T], BF16) for L in range(2)]
        rest = [sb(f"rest{L}", [P, 2, T]) for L in range(2)]
        stacked = [[sb(f"stacked{L}{h}", [P, SLOTS, 2, T], BF16) for h in range(2)] for L in range(2)]
        ones_bf = sb("ones_bf", [2, SLOTS, T], BF16)
        v_flat = [sb(f"v_flat{L}", [P, NT, C]) for L in range(2)]
        v_pad = [sb(f"v_pad{L}", [P, NT, HEADS, VW]) for L in range(2)]
        neg_max = [sb("neg_max0", [P, 3, GH]), sb("neg_max1", [P, 2, GH])]
        max_parts = [sb(f"max_parts{L}", [P, NT, 2, GH], BF16) for L in range(2)]
        max_rows = sb("max_rows", [2 * GH, T], BF16)
        probs = [sb(f"probs{n}", [P, GH, NT, T]) for n in range(2)]
        y_sb = [sb(f"y_sb{L}", [P, T]) for L in range(2)]
        y_inv = [sb(f"y_inv{L}", [P, NT, GH, 1]) for L in range(2)]
        y_norm = [sb(f"y_norm{L}", [P, NT, HEADS, HD]) for L in range(2)]
        yT = [sb(f"yT{L}", [P, T]) for L in range(2)]
        h3 = sb("h3", [P, T])

        X1 = sb("X1", [P, TILES, C])
        XF = sb("XF", [P, TILES, C])
        H3 = [sb(f"H3_{part}", [P, TILES * P], F32R) for part in ("high", "low")]
        LG = sb("LG", [P, TILES, E])
        MOD = sb("MOD", [P, B, 6, C])

        top = sb("top", [P, TILES, TOPK_W])
        top_i = sb("top_i", [P, TILES, TOPK_W], U32)
        top_f = sb("top_f", [P, TILES, 2])
        iota_e = sb("iota_e", [P, E])
        t_dif = sb("t_dif", [P, TILES, 1])
        t_exp = sb("t_exp", [P, TILES, 1])
        t_sum = sb("t_sum", [P, TILES, 1])
        w_top = sb("w_top", [P, 2, TILES, 1])
        pick = sb("pick", [P, 2, TILES, E])
        EW = sb("EW", [P, TILES, E])
        ewT = sb("ewT", [E, TILES * P])
        b1_e = [sb(f"b1_e{n}", [P, NJ]) for n in range(2)]
        W1 = [sb(f"W1_{n}", [P, DFF]) for n in range(2)]
        W2 = [sb(f"W2_{n}", [P, NJ, C]) for n in range(2)]
        NCH = TILES * P // 512
        W1p = [[sb(f"W1_{part}{n}", [P, DFF], F32R) for part in ("high", "low")] for n in range(2)]
        W2p = [[sb(f"W2_{part}{n}", [P, NJ, C], F32R) for part in ("high", "low")] for n in range(2)]
        PRODUCTS = [(0, 0), (0, 1), (1, 0)]
        HALF_T = TILES * P // 2
        moeT = [v_pad[n][:, :, :, :].rearrange("p t h w -> p (t h w)") for n in range(2)]
        weighted = [rest[n][:, :, :].rearrange("p n t -> p (n t)") for n in range(2)]
        ew_bc = probs[1][:, :, :, :].rearrange("p (n j) t q -> p n (j t q)", n=2)
        hid = probs[0][:, :, :, :].rearrange("p j t q -> p j (t q)")
        hidp = [[stacked[L][h][:, :, :, :].rearrange("p (j a) b t -> p j (a b t)", j=NJ).bitcast(F32R) for h in range(2)]
                for L in range(2)]

        bank = [pb(f"bank{n}", [P, 512]) for n in range(8)]
        row_bank, col_bank, av_bank, max_bank = bank[0:2], bank[2:4], bank[4], bank[5]
        small = bank[6:8]
        max_rows_ps = max_bank[:, :].bitcast(BF16)

        params_in = sem("params_in")
        consts = sem("consts")
        stacked_zero = sem("stacked_zero")
        dve_setup = sem("dve_setup")
        act_setup = sem("act_setup")
        pe_setup = sem("pe_setup")
        pool_setup = sem("pool_setup")
        mod_out = sem("mod_out")
        passed = sem("passed")
        x0_landed = sem("x0_landed")
        x_landed = sem("x_landed")
        mod0_landed = sem("mod0_landed")
        mod_landed = sem("mod_landed")
        stats_done = [sem(f"stats_done{n}") for n in range(4)]
        aggr_done = [sem(f"aggr_done{n}") for n in range(4)]
        eps_done = [sem(f"eps_done{n}") for n in range(4)]
        rstd_done = [sem(f"rstd_done{n}") for n in range(4)]
        norm_done = [sem(f"norm_done{n}") for n in range(4)]
        scale_done = [sem(f"scale_done{n}") for n in range(2)]
        shift_done = [sem(f"shift_done{n}") for n in range(2)]
        high_done = sems("high_done")
        mid_done = sems("mid_done")
        low_done = sems("low_done")
        half_landed = [sems(f"half{h}_landed") for h in range(2)]
        v_half_done = [sems(f"v_half{h}_done") for h in range(2)]
        small_full = sems("small_full")
        small_free = sems("small_free")
        rows_full = sem("rows_full")
        rows_free = sem("rows_free")
        cols_full = sem("cols_full")
        cols_free = sem("cols_free")
        max_split = sems("max_split")
        max_step = sems("max_step")
        maxT_full = sem("maxT_full")
        maxT_free = sem("maxT_free")
        shift_landed = sem("shift_landed")
        av_full = sem("av_full")
        y_sb_done = sem("y_sb_done")
        inv_done = sems("inv_done")
        y_norm_done = sems("y_norm_done")
        gabo_done = sem("gabo_done")
        x_gabo_done = sem("x_gabo_done")
        x1_done = sem("x1_done")
        xf_kept = sem("xf_kept")
        h3_free = sem("h3_free")
        top_step = sem("top_step")
        ew_exp = sem("ew_exp")
        ewT_full = sem("ewT_full")
        ewT_done = sem("ewT_done")
        ew_out = sem("ew_out")
        ew_landed = [sem(f"ew_landed{h}") for h in range(2)]
        b2_full = sem("b2_full")
        b2_kept = sem("b2_kept")
        weighted_done = sem("weighted_done")
        moe_T_full = sem("moe_T_full")
        moe_added = sem("moe_added")
        w_landed = [sem(f"w_landed{n}") for n in range(2)]
        cols_e = sem("cols_e")
        up_full = sem("up_full")
        w_high = [sem(f"w_high{n}") for n in range(2)]
        w_split = [sem(f"w_split{n}") for n in range(2)]
        h3_high = sem("h3_high")
        hid_high = sem("hid_high")
        hid_low = sem("hid_low")
        down_full = sem("down_full")
        acc_done = sem("acc_done")
        gated = sem("gated")
        final = sem("final")
        stored = sem("stored")

        x_v = x_dram.rearrange("b (t p) c -> p (b t) c", p=P)
        out_v = out.rearrange("b (t p) c -> p (b t) c", p=P)
        w1_v = io["L0_ffn_W1"]
        w2_v = io["L0_ffn_W2"].rearrange("e (j p) c -> e p j c", p=P)
        EXPERT_LOOP = E // 2

        def row(v):
            return v.rearrange("(o c) -> o c", o=1)

        def x_of(b):
            return X1[:, bass.ds(b * NT, NT), :]

        def mod_of(b, m):
            return MOD[:, bass.ds(b, 1), m, :].to_broadcast([P, NT, C])

        def bcast(ap, n=NT):
            return ap[:, None, :].to_broadcast([P, n, C])

        def over_iterations(eng, body):
            for i in range(-1, LOOP[0]):
                body(i)
            with eng.Fori(LOOP[0], LOOP[1]) as i:
                body(i)
            for i in range(LOOP[1], B + 3):
                body(i)

        def over_experts(eng, body):
            body(0)
            with eng.Fori(1, EXPERT_LOOP) as m:
                body(m)

        block = ctx.enter_context(nc.Block())

        @block.sync
        def _(sp):
            loads = [
                (c_rows[:, :], io["L0_c"]), (wmod[:, :], io["L0_wmod"]),
                (w_in[0][:, 0:C], io["L0_attn_Wq"]), (w_in[0][:, C:2 * C], io["L0_attn_Wk"]),
                (w_in[0][:, 2 * C:3 * C], io["L0_attn_Wv"]), (w_in[1][:, :], io["L0_ffn_w_qkv"]),
                (w_out[0][:, :], io["L0_attn_Wo"]), (w_out[1][:, :], io["L0_ffn_w_o"]),
                (gate_w[:, :], io["L0_ffn_gate_w"]),
                (qk_rows[0:1, :], row(io["L0_attn_bq"])), (qk_rows[1:2, :], row(io["L0_attn_bk"])),
                (qk_rows[2:4, :], io["L0_ffn_b_qkv"][0:2 * C].rearrange("(r c) -> r c", r=2)),
                (vec_rows[BV0:BV0 + 1, :], row(io["L0_attn_bv"])),
                (vec_rows[BV1:BV1 + 1, :], row(io["L0_ffn_b_qkv"][2 * C:3 * C])),
                (vec_rows[G1:G1 + 1, :], row(io["L0_ffn_ln1_g"])), (vec_rows[B1_:B1_ + 1, :], row(io["L0_ffn_ln1_b"])),
                (vec_rows[G2:G2 + 1, :], row(io["L0_ffn_ln2_g"])), (vec_rows[B2_:B2_ + 1, :], row(io["L0_ffn_ln2_b"])),
                (vec_rows[NV:NV + E * NJ, :], io["L0_ffn_b1"].rearrange("e (j p) -> (e j) p", p=P)),
                (b2_rows[:, :], io["L0_ffn_b2"]),
                (gate_b[:, :], row(io["L0_ffn_gate_b"]).to_broadcast([P, E])),
                (bo_bc[0][:, :], row(io["L0_attn_bo"]).to_broadcast([P, C])),
                (bo_bc[1][:, :], row(io["L0_ffn_b_o"]).to_broadcast([P, C])),
            ]
            for dst, src in loads:
                sp.dma_start(dst, src).then_inc(params_in, 16)
            sp.dma_start(X1[:, 0:NT, :], x_v[:, 0:NT, :]).then_inc(x0_landed, 16)
            sp.dma_start(X1[:, NT:TILES, :], x_v[:, NT:TILES, :]).then_inc(x_landed, 16)
            assert len(loads) == PARAMS
            sp.wait_ge(consts, CONSTS)
            sp.wait_ge(stacked_zero, 4)
            for L in range(2):
                for h in range(2):
                    sp.dma_start(stacked[L][h][QROWS:SROWS, :, 1, :], ones_bf[:, :, :]).then_inc(half_landed[h][L], 16)
            sp.wait_ge(dve_setup, SETUP_MOD)
            sp.dma_start(mod_dram, mod[:, :, :].rearrange("b m c -> b (m c)")).then_inc(mod_out, 16)
            sp.wait_ge(mod_out, 16)
            for b in range(B):
                sp.dma_start(MOD[:, b, :, :].rearrange("p m c -> p (m c)"),
                             mod_dram[b:b + 1, :].to_broadcast([P, 6 * C])).then_inc(mod_landed if b else mod0_landed, 16)

            def stack(L, b, h):
                at_least(sp, low_done[L], b + 1)
                if not isinstance(b, int) or b > 0:
                    sp.wait_ge(cols_full, 4 * place_of(L, b - 1, 2 * h + 1) + 4)
                for n, (qp, kp) in enumerate(PAIRS):
                    src = parts[L][64 * h:64 * h + 64, qp:4 + kp:3 + kp - qp, :]
                    dst = stacked[L][h][HD * n:HD * (n + 1), :, :, :]
                    sp.dma_start(dst, src).then_inc(half_landed[h][L], 16)

            def body(i):
                for turn in range(TURNS):
                    if turn == 3 and live(i + 1):
                        stack(0, i + 1, 0)
                    if turn == 2 and live(i - 2):
                        stack(1, i - 2, 1)
                    if turn == 6 and live(i - 1):
                        stack(1, i - 1, 0)
                    if turn == 6 and live(i + 1):
                        stack(0, i + 1, 1)

            def load_weights(m, n):
                at_least(sp, w_split[n], m * 2)
                sp.dma_start(W1[n][:, :], w1_v[bass.ds(m * 2 + n, 1)].rearrange("o p f -> (o p) f")).then_inc(w_landed[n], 16)
                sp.dma_start(W2[n][:, :, :], w2_v[bass.ds(m * 2 + n, 1)].rearrange("o p j c -> (o p) j c")).then_inc(w_landed[n], 16)
            load_weights(0, 0)
            load_weights(0, 1)

            over_iterations(sp, body)

            sp.wait_ge(ewT_done, TILES // 4)
            sp.dma_start(ew_dram, ewT[:, :]).then_inc(ew_out, 16)
            sp.wait_ge(ew_out, 16)

            def load_experts(m):
                for n in range(2):
                    e = m * 2 + n
                    if not isinstance(m, int):
                        load_weights(m, n)
                    for h in range(2):
                        at_least(sp, weighted_done, (e - 1) * NCH + 2 * h + 2)
                        sp.dma_start(ew_bc[:, h, :], ew_dram[bass.ds(e, 1), HALF_T * h:HALF_T * (h + 1)].to_broadcast([P, HALF_T])
                                     ).then_inc(ew_landed[h], 16)
            over_experts(sp, load_experts)
            for ch in range(NCH):
                sp.wait_ge(final, ch + 1)
                sp.dma_start(out_v[:, 4 * ch:4 * ch + 4, :], X1[:, 4 * ch:4 * ch + 4, :]).then_inc(stored, 16)
            sp.wait_ge(stored, 16 * NCH)

        @block.gpsimd
        def _(pool):
            pool.memset(zeros[:, :], 0.0).then_inc(pool_setup, 1)
            pool.memset(eps[:, :], EPS).then_inc(consts, 1)
            pool.memset(minus_half[:, :], -0.5).then_inc(consts, 1)
            pool.memset(ones_bf[:, :, :], 1.0).then_inc(consts, 1)
            pool.iota(iota_e[:, :], pattern=[[1, E]], base=0, channel_multiplier=0,
                      allow_small_or_imprecise_dtypes=True).then_inc(consts, 1)
            for L in range(2):
                pool.memset(v_pad[L][:, :, :, :], 0.0).then_inc(pool_setup, 1)
            pool.wait_ge(pool_setup, 3)
            for L in range(2):
                pool.memset(v_pad[L][:, :, :, HD:HD + 1], 1.0).then_inc(consts, 1)
            pool.affine_select(out=ident[:, :], in_=zeros[:, :], compare_op=ALU.not_equal, fill=1.0, base=0,
                               pattern=[[-1, P]], channel_multiplier=1).then_inc(pool_setup, 1)
            pool.wait_ge(pool_setup, 4)
            pool.tensor_copy(ident_bf[:, :], ident[:, :]).then_inc(consts, 1)
            pool.affine_select(out=mask_qk[:, :], in_=zeros[:, :], compare_op=ALU.is_ge, fill=MASKED, base=0,
                               pattern=[[-1, P]], channel_multiplier=1).then_inc(consts, 1)
            pool.affine_select(out=mask_kq[:, :], in_=zeros[:, :], compare_op=ALU.is_ge, fill=MASKED, base=0,
                               pattern=[[1, P]], channel_multiplier=-1).then_inc(consts, 1)

            pool.sem_inc(h3_free, 1)

            def alone(s, value):
                pool.wait_ge(s, value)
                pool.sem_inc(passed, 1)

            def rstd_of(n, b):
                pool.wait_ge(aggr_done[n], 2 * b + 2)
                pool.tensor_tensor(var_eps[:, n, :], mean_var[:, n, :, 1], eps[:, :], ALU.add).then_inc(eps_done[n], 1)
                pool.wait_ge(eps_done[n], b + 1)
                pool.tensor_tensor(rstd[:, n, :], var_eps[:, n, :], minus_half[:, :], ALU.pow).then_inc(rstd_done[n], 1)

            def modulate(n, b, m, dst):
                pool.wait_ge(norm_done[n], 2 * b + 2)
                pool.tensor_tensor(xm[n][:, :, :], xn[n][:, :, :], mod_of(b, m + 1), ALU.mult).then_inc(scale_done[n], 1)
                pool.wait_ge(scale_done[n], b + 1)
                pool.tensor_tensor(dst[:, :, :], xm[n][:, :, :], mod_of(b, m), ALU.add).then_inc(shift_done[n], 1)

            def low(L, b):
                pool.wait_ge(mid_done[L], b + 1)
                pool.tensor_tensor(parts[L][:, 2:6:3, :], rest[L][:, :, :], parts[L][:, 1:5:3, :],
                                   ALU.subtract).then_inc(low_done[L], 1)

            def v_half(L, b, h, i):
                if not isinstance(b, int) or b > 0:
                    pool.wait_ge(av_full, place_of(L, b - 1, 2 * h + 1) + 1)
                alone(small_free[L], bank_place(L, i, "v"))
                hs = slice(SLOTS * h, SLOTS * (h + 1))
                pool.tensor_copy(v_pad[L][:, :, hs, 0:HD],
                                 v_flat[L][:, :, :].rearrange("p t (h d) -> p t h d", d=HD)[:, :, hs, :]).then_inc(v_half_done[h][L], 1)

            def body(i):
                for turn in range(TURNS):
                    if turn == 0:
                        if live(i + 1):
                            rstd_of(0, i + 1)
                        if live(i - 1):
                            b = i - 1
                            pool.tensor_tensor(gabo[:, :], MOD[:, bass.ds(b, 1), GA, :].rearrange("p o c -> p (o c)"), bo_bc[0][:, :], ALU.mult).then_inc(gabo_done, 1)
                            pool.wait_ge(gabo_done, b + 1)
                            pool.tensor_tensor(x_gabo[:, :, :], x_of(b), bcast(gabo[:, :]), ALU.add).then_inc(x_gabo_done, 1)
                        if live(i + 1):
                            if is_first(i, -1):
                                pool.wait_ge(mod0_landed, 16)
                            if is_first(i, 0):
                                pool.wait_ge(mod_landed, 16 * (B - 1))
                            modulate(0, i + 1, SA, h_a)
                        if live(i):
                            v_half(0, i, 1, i - 1)
                    if turn == 1 and live(i - 1):
                        b = i - 1
                        rstd_of(1, b)
                        modulate(1, b, SB_, xf)
                    if turn == 2:
                        if live(i - 1):
                            b = i - 1
                            rstd_of(2, b)
                            pool.wait_ge(shift_done[1], b + 1)
                            pool.tensor_tensor(XF[:, bass.ds(b * NT, NT), :], xf[:, :, :], bcast(bo_bc[1][:, :]),
                                               ALU.add).then_inc(xf_kept, 1)
                    if turn == 3:
                        if live(i + 1):
                            low(0, i + 1)
                        if live(i - 2):
                            v_half(1, i - 2, 1, i - 1)
                    if turn == 4 and live(i + 1):
                        v_half(0, i + 1, 0, i)
                    if turn == 5:
                        if live(i - 1):
                            low(1, i - 1)
                        if is_first(i, B):
                            split_experts(0)
                    if turn == 6 and live(i - 3):
                        rstd_of(3, i - 3)
                    if turn == 7:
                        if live(i - 1):
                            v_half(1, i - 1, 0, i)
                        if live(i - 3):
                            alone(small_free[1], bank_place(1, i, "h3T"))
                            high, low_ = (H3[part][:, bass.ds((i - 3) * T, T)] for part in range(2))
                            pool.tensor_copy(high, h3[:, :]).then_inc(h3_high, 1)
                            pool.wait_ge(h3_high, i - 2)
                            pool.tensor_tensor(low_, h3[:, :], high, ALU.subtract).then_inc(h3_free, 1)

            def split_experts(m):
                for n in range(2):
                    at_least(pool, down_full, (m * 2 + n - 1) * NCH)
                    alone(w_landed[n], m * 32 + 32)
                    pool.tensor_copy(W1p[n][0][:, :], W1[n][:, :]).then_inc(w_high[n], 1)
                    pool.tensor_copy(W2p[n][0][:, :, :], W2[n][:, :, :]).then_inc(w_high[n], 1)
                    pool.wait_ge(w_high[n], m * 2 + 2)
                    pool.tensor_tensor(W1p[n][1][:, :], W1[n][:, :], W1p[n][0][:, :], ALU.subtract).then_inc(w_split[n], 1)
                    pool.tensor_tensor(W2p[n][1][:, :, :], W2[n][:, :, :], W2p[n][0][:, :, :], ALU.subtract).then_inc(w_split[n], 1)

            over_iterations(pool, body)

            with pool.Fori(1, EXPERT_LOOP) as m:
                split_experts(m)

            for ch in range(NCH):
                tiles = slice(4 * ch, 4 * ch + 4)
                pool.wait_ge(gated, ch + 1)
                pool.tensor_tensor(X1[:, tiles, :], X1[:, tiles, :], XF[:, tiles, :], ALU.add).then_inc(final, 1)

        @block.scalar
        def _(act):
            act.wait_ge(params_in, 16 * PARAMS)
            act.activation(silu_e[:, :], c_rows[:, :], ACT.Exp, scale=-1.0).then_inc(act_setup, 1)
            act.wait_ge(pe_setup, 1)
            act.activation(qk_bias[:, :], max_bank[:, 0:4], ACT.Copy).then_inc(act_setup, 1)
            act.activation(vec[:, :], max_bank[:, 64:64 + NV + E * NJ], ACT.Copy).then_inc(act_setup, 1)
            act.activation(silu_cT[:, :], max_bank[:, 256:256 + B], ACT.Copy).then_inc(act_setup, 1)
            act.wait_ge(act_setup, 4)

            def exps(i, turn, c):
                L, b, g = group_at(i, turn)
                if not live(b):
                    return
                n = 4 * place_of(L, b, g) + c
                act.wait_ge(cols_full, n + 1)
                width = [T + P, 2 * T][L]
                p = probs[probs_of(L, b, g)][:, c, :, :].rearrange("p t q -> p (t q)")
                act.activation(p[:, 0:width], col_bank[c % 2][:, 0:width], ACT.Exp, scale=SCALE).then_inc(cols_free, 1)

            def max_to_rows(i, turn):
                L, b, g = group_at(i, turn)
                if not live(b):
                    return
                n = place_of(L, b, g)
                act.wait_ge(maxT_full, n + 1)
                at_least(act, shift_landed, 16 * n)
                act.activation(max_rows[:, :], max_rows_ps[0:2 * GH, 0:T], ACT.Copy).then_inc(maxT_free, 1)

            def shift_rows(i, turn):
                L, b, g = group_at(i, turn)
                if not live(b):
                    return
                h, s = g // 2, GH * (g % 2)
                act.wait_ge(maxT_free, place_of(L, b, g) + 1)
                dst = stacked[L][h][QROWS:SROWS, s:s + GH, 0, :]
                act.dma_start(dst, max_rows[:, :]).then_inc(shift_landed, 16)

            def y_out(i, turn):
                L, b, g = group_at(i, turn)
                if not live(b):
                    return
                n = place_of(L, b, g)
                act.wait_ge(av_full, n + 1)
                act.activation(y_sb[L][:, :], av_bank[:, 0:T], ACT.Copy).then_inc(y_sb_done, 1)

            def hT_out(L, b, i):
                act.wait_ge(small_full[L], bank_place(L, i, "xT"))
                if L == 0:
                    act.activation(hT[0][:, :], small[0][:, 0:T], ACT.Copy).then_inc(small_free[0], 1)
                else:
                    act.activation(hT[1][:, :], small[1][:, 0:T], ACT.Identity, bias=vec[:, B1_:B1_ + 1],
                                   scale=vec[:, G1:G1 + 1]).then_inc(small_free[1], 1)

            def high(L, b, i):
                act.wait_ge(small_full[L], bank_place(L, i, "qk"))
                at_least(act, half_landed[1][L], 16 * (6 * b + 1))
                for n in range(2):
                    act.activation(parts[L][:, 3 * n, :], small[L][:, T * n:T * (n + 1)], ACT.Identity,
                                   bias=qk_bias[:, 2 * L + n:2 * L + n + 1]).then_inc(high_done[L], 1)

            def mid(L, b, i):
                act.wait_ge(small_free[L], bank_place(L, i, "qk"))
                act.activation(parts[L][:, 1:5:3, :], rest[L][:, :, :], ACT.Copy).then_inc(mid_done[L], 1)

            def v_out(L, b, i):
                act.wait_ge(small_full[L], bank_place(L, i, "v"))
                at_least(act, v_half_done[1][L], b)
                act.activation(v_flat[L][:, :, :].rearrange("p t c -> p (t c)"), small[L][:, 0:T], ACT.Copy).then_inc(small_free[L], 1)

            def yT_out(L, b, i):
                act.wait_ge(small_full[L], bank_place(L, i, "y2T"))
                act.activation(yT[L][:, :], small[L][:, 0:T], ACT.Identity,
                               bias=vec[:, BV0 + L:BV0 + L + 1]).then_inc(small_free[L], 1)

            def body(i):
                for turn in range(TURNS):
                    for c in range(GH):
                        exps(i, turn, c)
                        if c == 2:
                            y_out(i, turn - 1)
                        if c == 3:
                            max_to_rows(i, turn + 2)
                            shift_rows(i, turn + 2)
                        at = (turn, c)
                        if at == (0, 3) and live(i - 1):
                            yT_out(0, i - 1, i)
                        if at == (1, 3) and live(i + 1):
                            hT_out(0, i + 1, i)
                        if at == (4, 3) and live(i - 3):
                            yT_out(1, i - 3, i)
                        if at == (2, 1) and live(i + 1):
                            high(0, i + 1, i)
                        if at == (3, 0) and live(i + 1):
                            mid(0, i + 1, i)
                        if at == (2, 3) and live(i + 1):
                            v_out(0, i + 1, i)
                        if at == (6, 3) and live(i - 3):
                            act.wait_ge(small_full[1], bank_place(1, i, "h3T"))
                            at_least(act, h3_free, i - 2)
                            act.activation(h3[:, :], small[1][:, 0:T], ACT.Identity, bias=vec[:, B2_:B2_ + 1],
                                           scale=vec[:, G2:G2 + 1]).then_inc(small_free[1], 1)
                        if at == (3, 3) and live(i - 1):
                            hT_out(1, i - 1, i)
                        if at == (4, 1) and live(i - 1):
                            high(1, i - 1, i)
                        if at == (4, 3) and live(i - 1):
                            mid(1, i - 1, i)
                        if at == (5, 2) and live(i - 1):
                            v_out(1, i - 1, i)

            over_iterations(act, body)

            act.wait_ge(top_step, TOP_DIF)
            act.activation(t_exp[:, :, :], t_dif[:, :, :], ACT.Exp).then_inc(ew_exp, 1)

            def ewT_out():
                for q in range(TILES // 4):
                    act.wait_ge(ewT_full, q + 1)
                    act.activation(ewT[:, 512 * q:512 * q + 512], small[q % 2][0:E, :], ACT.Copy).then_inc(ewT_done, 1)

            def relus(m):
                for n in range(2):
                    e = m * 2 + n
                    for ch in range(NCH):
                        for j in range(NJ):
                            act.wait_ge(up_full, (e * NCH + ch) * NJ + j + 1)
                            if ch == 0 and j == 0:
                                act.wait_ge(cols_e, e + 1)
                            at_least(act, hid_low, (e * NCH + ch - 1) * NJ + j + 1)
                            act.activation(hid[:, j, :], bank[j][:, :], ACT.Relu, bias=b1_e[n][:, j:j + 1])
                            if j == 0:
                                at_least(act, down_full, e * NCH + ch - 1)
                            act.activation(hidp[ch % 2][0][:, j, :], bank[j][:, :], ACT.Relu,
                                           bias=b1_e[n][:, j:j + 1]).then_inc(hid_high, 1)
                        if is_first(m, 0) and n == 0 and ch == 0:
                            ewT_out()

            over_experts(act, relus)

        @block.vector
        def _(dve):
            for L in range(2):
                for h in range(2):
                    dve.memset(stacked[L][h][:, :, :, :], 0.0).then_inc(stacked_zero, 1)
            dve.wait_ge(params_in, 16 * PARAMS)
            steps = [0]

            def link(ins):
                steps[0] += 1
                ins.then_inc(dve_setup, 1)
                dve.wait_ge(dve_setup, steps[0])

            def permuted(dst, src):
                return (dst.rearrange("p (a d s) -> p a s d", a=2, d=HD), src.rearrange("p (a s d) -> p a s d", a=2, s=SLOTS))
            for L in range(2):
                for n in range(2):
                    for a in range(2):
                        o, s = permuted(w_qk[L][:, n, :], w_in[L][:, C * n:C * (n + 1)])
                        dve.tensor_copy(o[:, a], s[:, a])
            for a in range(2):
                o, s = permuted(qk_rows_p[:, :], qk_rows[:, :])
                ins = dve.tensor_copy(o[:, a], s[:, a])
            link(ins)
            dve.wait_ge(act_setup, 1)
            link(dve.tensor_scalar(silu_r[:, :], silu_e[:, :], 1.0, None, ALU.add))
            link(dve.reciprocal(silu_e[:, :], silu_r[:, :]))
            link(dve.tensor_tensor(silu_c[:, :], c_rows[:, :], silu_e[:, :], ALU.mult))
            assert steps[0] == SETUP_SILU
            dve.wait_ge(pe_setup, 2)
            m2 = mod[:, :, :].rearrange("b m c -> b (m c)")
            dve.tensor_copy(m2[:, 0:512], bank[0][0:B, :])
            link(dve.tensor_copy(m2[:, 512:768], bank[1][0:B, 0:256]))
            for m in (CA, CB):
                link(dve.tensor_scalar(mod[:, m, :], mod[:, m, :], 1.0, None, ALU.add))
            gates = mod[:, GA:GB + 1:GB - GA, :]
            link(dve.tensor_scalar(mod_sign[:, :, :], gates, 0.0, 2.0, ALU.is_ge, ALU.mult))
            link(dve.tensor_scalar(mod_sign[:, :, :], mod_sign[:, :, :], -1.0, None, ALU.add))
            link(dve.scalar_tensor_tensor(out=mod_abs[:, :, :], in0=gates, scalar=-1.0, in1=gates, op0=ALU.mult, op1=ALU.max))
            link(dve.scalar_tensor_tensor(out=gates, in0=mod_abs[:, :, :], scalar=0.25, in1=mod_sign[:, :, :],
                                          op0=ALU.max, op1=ALU.mult))
            assert steps[0] == SETUP_MOD

            def alone(s, value):
                dve.wait_ge(s, value)
                dve.sem_inc(passed, 1)

            def x_tile(b, t):
                return X1[:, bass.ds(b * NT + t, 1), :].rearrange("p o c -> p (o c)")

            def xf_tile(b, t):
                return xf[:, t, :]

            def xf2_tile(b, t):
                return XF[:, bass.ds(b * NT + t, 1), :].rearrange("p o c -> p (o c)")

            def norm_stats(n, b, src):
                for t in range(NT):
                    dve.bn_stats(stats[:, n, t, :], src(b, t)).then_inc(stats_done[n], 1)
                alone(stats_done[n], 2 * b + 2)
                for t in range(NT):
                    dve.bn_aggr(mean_var[:, n, t, :], stats[:, n, t, :]).then_inc(aggr_done[n], 1)

            def normalize(n, b, src):
                dve.wait_ge(rstd_done[n], b + 1)
                dve.wait_ge(aggr_done[n], 2 * b + 2)
                for t in range(NT):
                    dve.tensor_scalar(xn[n][:, t, :], src(b, t), mean_var[:, n, t, 0:1], rstd[:, n, t:t + 1],
                                      ALU.subtract, ALU.mult).then_inc(norm_done[n], 1)

            def row_max(i, turn, c):
                L, b, g = group_at(i, turn)
                if not live(b):
                    return
                n = 4 * place_of(L, b, g) + c
                dve.wait_ge(rows_full, n + 1)
                if c == 0:
                    at_least(dve, max_split[L], 2 * (4 * b + g))
                blocks, width = [(3, P), (2, T)][L]
                src = row_bank[c % 2][:, 0:blocks * width].rearrange("p (a k) -> p a k", a=blocks)
                dve.tensor_reduce(neg_max[L][:, :, c], src, AX.X, ALU.max, negate=True).then_inc(rows_free, 1)

            def split_max(i, turn):
                L, b, g = group_at(i, turn)
                if not live(b):
                    return
                n = 4 * b + g
                dve.wait_ge(rows_free, 4 * place_of(L, b, g) + 4)
                if L == 0:
                    dve.tensor_tensor(neg_max[0][:, 1, :], neg_max[0][:, 1, :], neg_max[0][:, 2, :],
                                      ALU.min).then_inc(max_step[0], 1)
                    dve.wait_ge(max_step[0], n + 1)
                if not isinstance(b, int) or n > 0:
                    pb_, pg = (b, g - 1) if g > 0 else (b - 1, GROUPS - 1)
                    dve.wait_ge(maxT_full, place_of(L, pb_, pg) + 1)
                dve.tensor_copy(max_parts[L][:, :, 0, :], neg_max[L][:, 0:2, :]).then_inc(max_split[L], 1)
                dve.wait_ge(max_split[L], 2 * n + 1)
                dve.tensor_tensor(max_parts[L][:, :, 1, :], neg_max[L][:, 0:2, :], max_parts[L][:, :, 0, :],
                                  ALU.subtract).then_inc(max_split[L], 1)

            def y_normalize(i, turn):
                L, b, g = group_at(i, turn)
                if not live(b):
                    return
                n = 4 * b + g
                dve.wait_ge(small_full[L], bank_place(L, i, "yT", g))
                ps = small[L][:, 0:T].rearrange("p (t c w) -> p t c w", t=NT, c=GH)
                dve.reciprocal(y_inv[L][:, :, :, :], ps[:, :, :, HD:HD + 1]).then_inc(inv_done[L], 1)
                dve.wait_ge(inv_done[L], n + 1)
                ins = None
                for t in range(NT):
                    ins = dve.tensor_tensor(y_norm[L][:, t, GH * g:GH * g + GH, :], ps[:, t, :, 0:HD],
                                            y_inv[L][:, t, :, :].to_broadcast([P, GH, HD]), ALU.mult)
                    if t == NT - 1:
                        ins.then_inc(small_free[L], 1)

            def rest_of(L, b, i):
                dve.wait_ge(high_done[L], 2 * b + 2)
                at_least(dve, low_done[L], b)
                for n in range(2):
                    ins = dve.scalar_tensor_tensor(out=rest[L][:, n, :], in0=small[L][:, T * n:T * (n + 1)],
                                                   scalar=qk_bias[:, 2 * L + n:2 * L + n + 1], in1=parts[L][:, 3 * n, :],
                                                   op0=ALU.add, op1=ALU.subtract)
                ins.then_inc(small_free[L], 1)

            def body(i):
                for turn in range(TURNS):
                    for c in range(GH):
                        row_max(i, turn + 3, c)
                        at = (turn, c)
                        if c == 1:
                            y_normalize(i, turn - 2)
                        if at == (0, 0) and live(i + 1):
                            if is_first(i, -1):
                                dve.wait_ge(x0_landed, 16)
                            if is_first(i, 0):
                                dve.wait_ge(x_landed, 16)
                            norm_stats(0, i + 1, x_tile)
                        if at == (0, 1) and live(i + 1):
                            at_least(dve, scale_done[0], i + 1)
                            normalize(0, i + 1, x_tile)
                        if at == (1, 1) and live(i - 1):
                            b = i - 1
                            dve.wait_ge(small_full[0], bank_place(0, i, "wo"))
                            if is_first(i, 1):
                                dve.wait_ge(mod_landed, 16 * (B - 1))
                            dve.tensor_tensor(attn_g[:, :, :], small[0][:, 0:T].rearrange("p (t c) -> p t c", t=NT),
                                              mod_of(b, GA), ALU.mult).then_inc(small_free[0], 1)
                            dve.wait_ge(small_free[0], bank_place(0, i, "wo"))
                            dve.wait_ge(x_gabo_done, b + 1)
                            dve.tensor_tensor(x_of(b), attn_g[:, :, :], x_gabo[:, :, :], ALU.add).then_inc(x1_done, 1)
                            alone(x1_done, b + 1)
                            norm_stats(1, b, x_tile)
                        if at == (1, 2) and live(i - 1):
                            at_least(dve, scale_done[1], i - 1)
                            normalize(1, i - 1, x_tile)
                        if at == (2, 2) and live(i + 1):
                            rest_of(0, i + 1, i)
                        if at == (2, 1) and live(i - 1):
                            dve.wait_ge(shift_done[1], i)
                            norm_stats(2, i - 1, xf_tile)
                        if at == (2, 3) and live(i - 1):
                            normalize(2, i - 1, xf_tile)
                        if at == (4, 2) and live(i - 1):
                            rest_of(1, i - 1, i)
                        if at == (6, 0) and live(i - 3):
                            b = i - 3
                            dve.wait_ge(small_full[1], bank_place(1, i, "wo"))
                            dve.wait_ge(xf_kept, b + 1)
                            rows = XF[:, bass.ds(b * NT, NT), :]
                            dve.tensor_tensor(rows, rows, small[1][:, 0:T].rearrange("p (t c) -> p t c", t=NT),
                                              ALU.add).then_inc(small_free[1], 1)
                            alone(small_free[1], bank_place(1, i, "wo"))
                            norm_stats(3, b, xf2_tile)
                        if at == (6, 2) and live(i - 3):
                            normalize(3, i - 3, xf2_tile)
                        if at == (7, 2) and live(i - 3):
                            b = i - 3
                            dve.wait_ge(small_full[1], bank_place(1, i, "gate"))
                            dve.tensor_tensor(LG[:, bass.ds(b * NT, NT), :],
                                              small[1][:, 0:NT * E].rearrange("p (t e) -> p t e", t=NT),
                                              gate_b[:, None, :].to_broadcast([P, NT, E]), ALU.add).then_inc(small_free[1], 1)
                    split_max(i, turn + 3)

            over_iterations(dve, body)

            made = [0]

            def then(ins):
                made[0] += 1
                ins.then_inc(top_step, 1)
                dve.wait_ge(top_step, made[0])
            dve.wait_ge(consts, CONSTS)
            for n in range(2):
                dve.tensor_copy(b1_e[n][:, :], vec[:, n * NJ + NV:(n + 1) * NJ + NV]).then_inc(cols_e, 1)
            dve.wait_ge(small_free[1], bank_place(1, B + 2, "gate"))
            for t in range(TILES):
                ins = dve.max(top[:, t, :], LG[:, t, :])
            then(ins)
            for t in range(TILES):
                dve.max_index(top_i[:, t, :], top[:, t, :], LG[:, t, :])
            ins = dve.tensor_tensor(t_dif[:, :, :], top[:, :, 1:2], top[:, :, 0:1], ALU.subtract)
            then(ins)
            assert made[0] == TOP_DIF
            then(dve.tensor_copy(top_f[:, :, :], top_i[:, :, 0:2]))
            dve.wait_ge(ew_exp, 1)
            then(dve.tensor_scalar(t_sum[:, :, :], t_exp[:, :, :], 1.0, None, ALU.add))
            then(dve.reciprocal(w_top[:, 0, :, :], t_sum[:, :, :]))
            then(dve.tensor_tensor(w_top[:, 1, :, :], w_top[:, 0, :, :], t_exp[:, :, :], ALU.mult))
            iotas = iota_e[:, None, :].to_broadcast([P, TILES, E])
            for k in range(2):
                then(dve.tensor_tensor(pick[:, k, :, :], iotas, top_f[:, :, k:k + 1].to_broadcast([P, TILES, E]), ALU.is_equal))
                then(dve.tensor_tensor(pick[:, k, :, :], pick[:, k, :, :], w_top[:, k, :, :].to_broadcast([P, TILES, E]), ALU.mult))
            then(dve.tensor_tensor(EW[:, :, :], pick[:, 0, :, :], pick[:, 1, :, :], ALU.add))
            assert made[0] == TOP_ALL

            def b2_out():
                for ch in range(NCH):
                    dve.wait_ge(b2_full, ch + 1)
                    dve.tensor_copy(moeT[ch // 2][:, 512 * (ch % 2):512 * (ch % 2) + 512], small[ch % 2][:, :]).then_inc(b2_kept, 1)
                dve.wait_ge(b2_kept, NCH)

            def accumulate(e, n, ch):
                dve.wait_ge(down_full, e * NCH + ch + 1)
                if ch % 2 == 0:
                    dve.wait_ge(ew_landed[ch // 2], 16 * e + 16)
                cols = slice(512 * (ch % 2), 512 * (ch % 2) + 512)
                at_least(dve, acc_done, e * NCH + ch - 1)
                dve.tensor_tensor(weighted[ch % 2], bank[4 + ch % 2][:, :], ew_bc[:, ch // 2, cols],
                                  ALU.mult).then_inc(weighted_done, 1)
                dve.wait_ge(weighted_done, e * NCH + ch + 1)
                at_least(dve, acc_done, (e - 1) * NCH + ch + 1)
                dve.tensor_tensor(moeT[ch // 2][:, cols], moeT[ch // 2][:, cols], weighted[ch % 2], ALU.add).then_inc(acc_done, 1)

            def lows(m):
                for n in range(2):
                    e = m * 2 + n
                    if not is_first(m, 0):
                        dve.tensor_copy(b1_e[n][:, :], vec[:, bass.ds(e * NJ + NV, NJ)]).then_inc(cols_e, 1)
                    for ch in range(NCH):
                        for j in range(NJ):
                            dve.wait_ge(hid_high, (e * NCH + ch) * NJ + j + 1)
                            dve.tensor_tensor(hidp[ch % 2][1][:, j, :], hid[:, j, :], hidp[ch % 2][0][:, j, :],
                                              ALU.subtract).then_inc(hid_low, 1)
                        if is_first(m, 0) and n == 0 and ch == 0:
                            b2_out()
                        if ch > 0:
                            accumulate(e, n, ch - 1)
                        elif not isinstance(e, int) or e > 0:
                            accumulate(e - 1, 1 - n, NCH - 1)
            over_experts(dve, lows)
            accumulate(E - 1, 1, NCH - 1)
            for ch in range(NCH):
                dve.wait_ge(moe_T_full, ch + 1)
                tiles = slice(4 * ch, 4 * ch + 4)
                dve.tensor_tensor(XF[:, tiles, :], XF[:, tiles, :], bank[ch][:, :].rearrange("p (t c) -> p t c", t=4),
                                  ALU.add).then_inc(moe_added, 1)
                dve.wait_ge(moe_added, ch + 1)
                f = XF[:, tiles, :].rearrange("p (b t) c -> p b t c", t=NT)
                g = MOD[:, 2 * ch:2 * ch + 2, GB:GB + 1, :].to_broadcast([P, 2, NT, C])
                dve.tensor_tensor(f, f, g, ALU.mult).then_inc(gated, 1)

        @block.tensor
        def _(pe):
            pe.wait_ge(consts, CONSTS)
            pe.wait_ge(dve_setup, SETUP_SILU)
            pe.transpose(max_bank[:, 0:4], qk_rows_p[:, :], ident[0:4, 0:4])
            nv = NV + E * NJ
            pe.transpose(max_bank[:, 64:64 + nv], vec_rows[:, :], ident[0:nv, 0:nv])
            pe.transpose(max_bank[:, 256:256 + B], silu_c[:, :], ident[0:B, 0:B]).then_inc(pe_setup, 1)
            pe.wait_ge(act_setup, 4)
            pe.matmul(bank[0][0:B, :], silu_cT[:, :], wmod[:, 0:512], start=True, stop=True)
            pe.matmul(bank[1][0:B, 0:256], silu_cT[:, :], wmod[:, 512:768], start=True, stop=True).then_inc(pe_setup, 1)
            pe.wait_ge(dve_setup, SETUP_SILU + 1)

            def scores_rows(i, turn, c):
                L, b, g = group_at(i, turn)
                if not live(b):
                    return
                n = 4 * place_of(L, b, g) + c
                h, s = g // 2, GH * (g % 2) + c
                if c == 0 and g % 2 == 0:
                    pe.wait_ge(half_landed[h][L], 16 * (1 + 6 * (b + 1)))
                at_least(pe, rows_free, n - 1)
                q, k = stacked[L][h][0:QROWS, s, 0, :], stacked[L][h][0:QROWS, s, 1, :]
                ps = row_bank[c % 2]
                if L == 0:
                    pe.matmul(ps[:, 0:P], q[:, 0:P], k[:, 0:P], start=True, stop=True)
                    pe.matmul(ps[:, 0:P], ident_bf[:, :], mask_qk[:, :], start=False, stop=True, skip_group_check=True)
                    pe.matmul(ps[:, P:3 * P], q[:, P:T], k[:, :], start=True, stop=True)
                    ins = pe.matmul(ps[:, 2 * P:3 * P], ident_bf[:, :], mask_qk[:, :], start=False, stop=True,
                                    skip_group_check=True)
                else:
                    pe.matmul(ps[:, 0:T], q[:, 0:P], k[:, :], start=True, stop=True)
                    ins = pe.matmul(ps[:, T:2 * T], q[:, P:T], k[:, :], start=True, stop=True)
                ins.then_inc(rows_full, 1)

            def scores_cols(i, turn, c):
                L, b, g = group_at(i, turn)
                if not live(b):
                    return
                n = 4 * place_of(L, b, g) + c
                h, s = g // 2, GH * (g % 2) + c
                if c == 0:
                    pe.wait_ge(shift_landed, 16 * (place_of(L, b, g) + 1))
                at_least(pe, cols_free, n - 1)
                q, k = stacked[L][h][:, s, 0, :], stacked[L][h][:, s, 1, :]
                ps = col_bank[c % 2]
                if L == 0:
                    pe.matmul(ps[:, 0:T], k[:, 0:P], q[:, :], start=True, stop=True)
                    pe.matmul(ps[:, 0:P], ident_bf[:, :], mask_kq[:, :], start=False, stop=True, skip_group_check=True)
                    pe.matmul(ps[:, T:T + P], k[:, P:T], q[:, P:T], start=True, stop=True)
                    ins = pe.matmul(ps[:, T:T + P], ident_bf[:, :], mask_kq[:, :], start=False, stop=True, skip_group_check=True)
                else:
                    pe.matmul(ps[:, 0:T], k[:, 0:P], q[:, :], start=True, stop=True)
                    ins = pe.matmul(ps[:, T:2 * T], k[:, P:T], q[:, :], start=True, stop=True)
                ins.then_inc(cols_full, 1)

            def max_transposes(i, turn):
                L, b, g = group_at(i, turn)
                if not live(b):
                    return
                n = place_of(L, b, g)
                pe.wait_ge(max_split[L], 2 * (4 * b + g) + 2)
                at_least(pe, maxT_free, n)
                for t in range(NT):
                    ins = pe.transpose(max_rows_ps[0:2 * GH, P * t:P * (t + 1)],
                                       max_parts[L][:, t, :, :].rearrange("p a c -> p (a c)"), ident_bf[:, :])
                ins.then_inc(maxT_full, 1)

            def weighted_values(i, turn):
                L, b, g = group_at(i, turn)
                if not live(b):
                    return
                n = place_of(L, b, g)
                pe.wait_ge(cols_free, 4 * n + 4)
                if g % 2 == 0:
                    pe.wait_ge(v_half_done[g // 2][L], b + 1)
                at_least(pe, y_sb_done, n)
                p = probs[probs_of(L, b, g)]
                for t in range(NT):
                    for c in range(GH):
                        ps = av_bank[VW * c:VW * (c + 1), 0:T]
                        v = v_pad[L][:, t, GH * g + c, :]
                        pc = p[:, c, :, :].rearrange("p t q -> p (t q)")
                        if L == 0 and t == 1:
                            ins = pe.matmul(ps[:, P:T], v, pc[:, T:T + P], start=False, stop=True,
                                            tile_position=(0, VW * c), skip_group_check=True)
                        else:
                            ins = pe.matmul(ps, v, pc[:, T * t:T * (t + 1)], start=(t == 0), stop=(t == 1),
                                            tile_position=(0, VW * c), skip_group_check=True)
                ins.then_inc(av_full, 1)

            def fill(L, place):
                if isinstance(place, int):
                    at_least(pe, small_free[L], place - 1)
                else:
                    pe.wait_ge(small_free[L], place - 1)

            def y_transposes(i, turn):
                L, b, g = group_at(i, turn)
                if not live(b):
                    return
                fill(L, bank_place(L, i, "yT", g))
                pe.wait_ge(y_sb_done, place_of(L, b, g) + 1)
                for t in range(NT):
                    ins = pe.transpose(small[L][:, P * t:P * (t + 1)], y_sb[L][:, P * t:P * (t + 1)], ident[:, :])
                ins.then_inc(small_full[L], 1)

            def tiles_T(L, i, what, src):
                for t in range(NT):
                    ins = pe.transpose(small[L][:, P * t:P * (t + 1)], src[:, t, :], ident[:, :])
                ins.then_inc(small_full[L], 1)

            def project_y(L, i, b):
                fill(L, bank_place(L, i, "wo"))
                for t in range(NT):
                    ins = pe.matmul(small[L][:, C * t:C * (t + 1)], yT[L][:, P * t:P * (t + 1)], w_out[L][:, :],
                                    start=True, stop=True)
                ins.then_inc(small_full[L], 1)

            def project_qk(L, i, b):
                fill(L, bank_place(L, i, "qk"))
                for n in range(2):
                    ins = pe.matmul(small[L][:, T * n:T * (n + 1)], w_qk[L][:, n, :], hT[L][:, :], start=True, stop=True)
                ins.then_inc(small_full[L], 1)

            def project_v(L, i, b):
                fill(L, bank_place(L, i, "v"))
                for t in range(NT):
                    ins = pe.matmul(small[L][:, C * t:C * (t + 1)], hT[L][:, P * t:P * (t + 1)],
                                    w_in[L][:, 2 * C:3 * C], start=True, stop=True)
                ins.then_inc(small_full[L], 1)

            def y2T(L, i, b):
                place = bank_place(L, i, "y2T")
                fill(L, place)
                tiles_T(L, i, "y2T", y_norm[L][:, :, :, :].rearrange("p t h d -> p t (h d)"))

            def body(i):
                for turn in range(TURNS):
                    for c in range(GH):
                        scores_cols(i, turn, c)
                        scores_rows(i, turn + 3, c)
                        at = (turn, c)
                        if c == 0:
                            y_transposes(i, turn - 2)
                        if c == 2:
                            max_transposes(i, turn + 2)
                        if c == 1:
                            weighted_values(i, turn - 1)
                        if at == (0, 2) and live(i - 1):
                            y2T(0, i, i - 1)
                        if at == (1, 0) and live(i - 1):
                            project_y(0, i, i - 1)
                        if at == (1, 2) and live(i + 1):
                            fill(0, bank_place(0, i, "xT"))
                            pe.wait_ge(shift_done[0], i + 2)
                            tiles_T(0, i, "xT", h_a)
                        if at == (4, 3) and live(i - 3):
                            y2T(1, i, i - 3)
                        if at == (5, 3) and live(i - 3):
                            project_y(1, i, i - 3)
                        if at == (2, 1) and live(i + 1):
                            project_qk(0, i, i + 1)
                        if at == (2, 3) and live(i + 1):
                            project_v(0, i, i + 1)
                        if at == (6, 3) and live(i - 3):
                            fill(1, bank_place(1, i, "h3T"))
                            pe.wait_ge(norm_done[3], 2 * (i - 3) + 2)
                            tiles_T(1, i, "h3T", xn[3])
                        if at == (3, 2) and live(i - 1):
                            fill(1, bank_place(1, i, "xT"))
                            pe.wait_ge(norm_done[2], 2 * (i - 1) + 2)
                            tiles_T(1, i, "xT", xn[2])
                        if at == (7, 1) and live(i - 3):
                            fill(1, bank_place(1, i, "gate"))
                            for t in range(NT):
                                ins = pe.matmul(small[1][:, E * t:E * (t + 1)], h3[:, P * t:P * (t + 1)], gate_w[:, :],
                                                start=True, stop=True)
                            ins.then_inc(small_full[1], 1)
                        if at == (4, 0) and live(i - 1):
                            project_qk(1, i, i - 1)
                        if at == (5, 1) and live(i - 1):
                            project_v(1, i, i - 1)

            over_iterations(pe, body)

            def second_biases():
                pe.wait_ge(top_step, TOP_ALL)
                for q in range(TILES // 4):
                    at_least(pe, ewT_done, q - 1)
                    for k in range(4):
                        ins = pe.transpose(small[q % 2][0:E, P * k:P * (k + 1)], EW[:, 4 * q + k, :], ident[:, :])
                    ins.then_inc(ewT_full, 1)
                for ch in range(NCH):
                    if ch < 2:
                        pe.wait_ge(ewT_done, ch + TILES // 4 - 1)
                    else:
                        pe.wait_ge(b2_kept, ch - 1)
                    pe.matmul(small[ch % 2][:, :], b2_rows[:, :], ewT[:, 512 * ch:512 * ch + 512],
                              start=True, stop=True).then_inc(b2_full, 1)

            pe.wait_ge(h3_free, B + 1)

            def up(e, n, ch):
                for j in range(NJ):
                    at_least(pe, hid_high, (e * NCH + ch - 1) * NJ + j + 1)
                    for p, (wp, hp) in enumerate(PRODUCTS):
                        ins = pe.matmul(bank[j][:, :], W1p[n][wp][:, P * j:P * (j + 1)],
                                        H3[hp][:, 512 * ch:512 * (ch + 1)], start=(p == 0), stop=(p == 2))
                    ins.then_inc(up_full, 1)

            def down(e, n, ch):
                at_least(pe, weighted_done, e * NCH + ch - 1)
                pe.wait_ge(hid_low, (e * NCH + ch + 1) * NJ)
                for j in range(NJ):
                    for p, (wp, hp) in enumerate(PRODUCTS):
                        ins = pe.matmul(bank[4 + ch % 2][:, :], W2p[n][wp][:, j, :], hidp[ch % 2][hp][:, j, :],
                                        start=(j == 0 and p == 0), stop=(j == NJ - 1 and p == 2))
                ins.then_inc(down_full, 1)

            def experts(m):
                for n in range(2):
                    e = m * 2 + n
                    pe.wait_ge(w_split[n], m * 2 + 2)
                    for ch in range(NCH):
                        up(e, n, ch)
                        if is_first(m, 0) and n == 0 and ch == 0:
                            second_biases()
                        if ch > 0:
                            down(e, n, ch - 1)
                        elif not isinstance(e, int) or e > 0:
                            down(e - 1, 1 - n, NCH - 1)

            over_experts(pe, experts)
            down(E - 1, 1, NCH - 1)
            for ch in range(NCH):
                pe.wait_ge(acc_done, (E - 1) * NCH + ch + 1)
                for k in range(4):
                    n = 4 * (ch % 2) + k
                    ins = pe.transpose(bank[ch][:, P * k:P * (k + 1)], moeT[ch // 2][:, P * n:P * (n + 1)], ident[:, :])
                ins.then_inc(moe_T_full, 1)


_INS = ['L0_attn_x', 'L0_attn_Wq', 'L0_attn_bq', 'L0_attn_Wk', 'L0_attn_bk', 'L0_attn_Wv', 'L0_attn_bv',
        'L0_attn_Wo', 'L0_attn_bo', 'L0_ffn_ln1_g', 'L0_ffn_ln1_b', 'L0_ffn_w_qkv', 'L0_ffn_b_qkv', 'L0_ffn_w_o',
        'L0_ffn_b_o', 'L0_ffn_ln2_g', 'L0_ffn_ln2_b', 'L0_ffn_gate_w', 'L0_ffn_gate_b', 'L0_ffn_W1', 'L0_ffn_b1',
        'L0_ffn_W2', 'L0_ffn_b2', 'L0_c', 'L0_wmod']


def kernel(**inputs):
    import numpy as _np
    import concourse.bacc as _bacc
    from concourse import mybir as _mybir
    from concourse.bass_utils import run_bass_kernel_spmd as _run

    nc = _bacc.Bacc("TRN2", target_bir_lowering=False, num_devices=1)
    arrays, io = {}, {}
    for name in _INS:
        a = _np.ascontiguousarray(inputs[name])
        arrays[f"in_{name}"] = a
        io[name] = nc.dram_tensor(f"in_{name}", a.shape, _mybir.dt.from_np(a.dtype), kind="ExternalInput").ap()
    batches = inputs["L0_c"].shape[0]
    out = nc.dram_tensor("out_0", inputs["L0_attn_x"].shape, _mybir.dt.float32, kind="ExternalOutput").ap()
    mod_dram = nc.dram_tensor("mod_rows", (batches, inputs["L0_wmod"].shape[1]), _mybir.dt.float32, kind="Internal").ap()
    batches, tokens, _ = inputs["L0_attn_x"].shape
    experts = inputs["L0_ffn_gate_w"].shape[1]
    ew_dram = nc.dram_tensor("ew_rows", (experts, batches * tokens), _mybir.dt.float32, kind="Internal").ap()
    build(nc, io, out, mod_dram, ew_dram)
    r = _run(nc, [arrays], core_ids=[0])
    return r.results[0]["out_0"]
```

```python
from contextlib import ExitStack

import concourse.bass as bass
from concourse import mybir

F32 = mybir.dt.float32
BF16 = mybir.dt.bfloat16
F32R = mybir.dt.float32r
U32 = mybir.dt.uint32
ALU = mybir.AluOpType
ACT = mybir.ActivationFunctionType
AX = mybir.AxisListType

P = 128
HD = 8
HEADS = 16
GH = 4
GROUPS = HEADS // GH
SLOTS = HEADS // 2
SHIFT = P - 2
VW = 32
TURNS = 2 * GROUPS
EPS = 1e-5
SCALE = HD ** -0.5
MASKED = -1e30
TOPK_W = 8
PAIRS = [(0, 0), (0, 1), (0, 2), (1, 0), (1, 1), (2, 0)]
SA, CA, GA, SB_, CB, GB = range(6)

PE_AT = {("y2T", 0): ((0, 1), -1), ("wo", 0): ((0, 3), -1), ("xT", 0): ((1, 2), 1), ("qk", 0): ((2, 1), 1),
         ("v", 0): ((3, 0), 1), ("xT", 1): ((3, 1), -1), ("qk", 1): ((4, 0), -1), ("y2T", 1): ((4, 3), -3),
         ("v", 1): ((5, 1), -1), ("wo", 1): ((5, 3), -3), ("h3T", 1): ((6, 3), -3), ("gate", 1): ((7, 3), -3)}
ACT_AT = {"yT0": (0, 1), "hT0": (1, 2), "high0": (2, 1), "v0": (3, 0), "mid0": (2, 2), "hT1": (3, 2),
          "high1": (4, 0), "mid1": (4, 3), "yT1": (4, 2), "v1": (5, 1), "h3": (6, 3)}
DVE_AT = {"stats0": (0, 0), "norm0": (0, 3), "x1": (0, 3), "norm1": (1, 2), "stats2": (2, 1), "norm2": (2, 3),
          "rest0": (2, 2), "rest1": (4, 1), "xf2": (5, 3), "norm3": (6, 1), "logits": (7, 3)}
YT_AT, MAXT_AT, AV_AT, Y_OUT_AT, MAX_AT, Y_NORM_AT = 0, 2, 1, 1, 3, 0
EARLY, LATE = 6, 15
CONSTS = 9
SETUP_SILU, SETUP_QK, SETUP_MOD, SETUP_QK1 = 3, 4, 11, 12
TOP_DIF, TOP_ALL = 2, 11


def at_least(eng, sem, value):
    if isinstance(value, int) and value <= 0:
        return
    eng.wait_ge(sem, value)


def build(nc, io, out, mod_dram, ew_dram):
    x_dram = io["L0_attn_x"]
    B, T, C = x_dram.shape
    E = io["L0_ffn_gate_w"].shape[1]
    DFF = io["L0_ffn_W1"].shape[2]
    NJ = DFF // P
    NT = T // P
    TILES = B * NT
    LAG = 2 * GROUPS + 1
    LOOP = (3, B - 1)
    assert C == P and NT == 2 and T == 256

    def live(b):
        return not isinstance(b, int) or 0 <= b < B

    def is_first(i, n):
        return isinstance(i, int) and i == n

    def group_at(i, turn):
        if turn < 0:
            i, turn = i - 1, turn + TURNS
        if turn >= TURNS:
            i, turn = i + 1, turn - TURNS
        k = turn // 2
        if turn % 2 == 0:
            return 0, i, k
        return (1, i - 3, GROUPS - 1) if k == 0 else (1, i - 2, k - 1)

    def place_of(L, b, g):
        n = GROUPS * b + g
        if L == 0:
            return n if isinstance(b, int) and n < LAG else 2 * n - LAG
        return 2 * n + LAG + 1 if not isinstance(b, int) or n < GROUPS * B - LAG else n + GROUPS * B

    def pair_of(L, b, g):
        n = place_of(L, b, g)
        if isinstance(n, int):
            return n // 2
        return GROUPS * b + g + [-1, 1][L] * (LAG + 1) // 2

    def probs_of(L, b, g):
        n = place_of(L, b, g)
        return n % 2 if isinstance(n, int) else (1 - L if LAG % 2 else L)

    def bank_uses(L, i):
        uses = []
        for turn in range(TURNS):
            for c in range(GH):
                if c == YT_AT and group_at(i, turn - 2)[0] == L:
                    uses.append(("yT",) + group_at(i, turn - 2)[1:])
                uses += [(what, i + later, 0) for (what, layer), (when, later) in PE_AT.items()
                         if layer == L and when == (turn, c)]
        return [u for u in uses if live(u[1])]

    def bank_place(L, i, what, g=0):
        n = i if isinstance(i, int) else LOOP[0]
        before = sum(len(bank_uses(L, m)) for m in range(-1, n))
        names = [(u[0], u[2]) for u in bank_uses(L, n)]
        here = before + names.index((what, g)) + 1
        if isinstance(i, int):
            return here
        return (i - LOOP[0]) * len(bank_uses(L, n)) + here

    ctx = ExitStack()
    with ctx:
        def sb(name, shape, dt=F32):
            return ctx.enter_context(nc.sbuf_tensor(name, shape, dt))

        def pb(name, shape, dt=F32):
            return ctx.enter_context(nc.psum_tensor(name, shape, dt))

        def sem(name):
            return ctx.enter_context(nc.semaphore(name))

        def sems(name):
            return [sem(f"{name}{L}") for L in range(2)]

        w_in = [sb("w_in0", [P, 3 * C]), sb("w_in1", [P, 3 * C])]
        w_qk = [sb(f"w_qk{L}", [P, 2, C]) for L in range(2)]
        w_out = [sb("w_out0", [P, C]), sb("w_out1", [P, C])]
        gate_w = sb("gate_w", [P, E])
        wmod = sb("wmod", [P, 6 * C])
        c_rows = sb("c_rows", [B, C])
        qk_rows = sb("qk_rows", [4, C])
        qk_rows_p = sb("qk_rows_p", [4, C])
        NV = 6
        vec_rows = sb("vec_rows", [NV + E * NJ, C])
        qk_bias = sb("qk_bias", [P, 4])
        vec = sb("vec", [P, NV + E * NJ])
        BV0, BV1, G1, B1_, G2, B2_ = range(NV)
        b2_rows = sb("b2_rows", [E, C])
        gate_b = sb("gate_b", [P, E])
        bo_bc = [sb("bo_bc0", [P, C]), sb("bo_bc1", [P, C])]
        ident = sb("ident", [P, P])
        ident_bf = sb("ident_bf", [P, P], BF16)
        zeros = sb("zeros", [P, P])
        mask_qk = sb("mask_qk", [P, P], BF16)
        mask_kq = sb("mask_kq", [P, P], BF16)
        eps = sb("eps", [P, NT])
        minus_half = sb("minus_half", [P, NT])
        silu_e = sb("silu_e", [B, C])
        silu_r = sb("silu_r", [B, C])
        silu_c = sb("silu_c", [B, C])
        silu_cT = sb("silu_cT", [P, B])
        mod = sb("mod", [B, 6, C])
        mod_sign = sb("mod_sign", [B, 2, C])
        mod_abs = sb("mod_abs", [B, 2, C])

        gabo = sb("gabo", [P, C])
        x_gabo = sb("x_gabo", [P, NT, C])
        attn_g = sb("attn_g", [P, NT, C])
        xf = sb("xf", [P, NT, C])
        stats = sb("stats", [P, 4, NT, 6])
        mean_var = sb("mean_var", [P, 4, NT, 2])
        var_eps = sb("var_eps", [P, 4, NT])
        rstd = sb("rstd", [P, 4, NT])
        xn = [sb(f"xn{n}", [P, NT, C]) for n in range(4)]
        xm = [sb(f"xm{n}", [P, NT, C]) for n in range(2)]
        h_a = sb("h_a", [P, NT, C])
        hT = [sb(f"hT{L}", [P, T]) for L in range(2)]
        parts = [sb(f"parts{L}", [P, 6, T], BF16) for L in range(2)]
        rest = [sb(f"rest{L}", [P, 2, T]) for L in range(2)]
        stacked = [[sb(f"stacked{L}{h}", [P, SLOTS, 2, T], BF16) for h in range(2)] for L in range(2)]
        ones_bf = sb("ones_bf", [2, SLOTS, T], BF16)
        v_flat = [sb(f"v_flat{L}", [P, NT, C]) for L in range(2)]
        v_pad = [sb(f"v_pad{L}", [P, NT, HEADS, VW]) for L in range(2)]
        neg_max = [sb("neg_max0", [P, 3, GH]), sb("neg_max1", [P, 2, GH])]
        max_parts = [sb(f"max_parts{L}", [P, NT, 2, GH], BF16) for L in range(2)]
        max_rows = [sb(f"max_rows{n}", [2 * GH, T], BF16) for n in range(2)]
        probs = [sb(f"probs{n}", [P, GH, NT, T]) for n in range(2)]
        y_sb = [sb(f"y_sb{L}", [P, T]) for L in range(2)]
        y_inv = [sb(f"y_inv{L}", [P, NT, GH, 1]) for L in range(2)]
        y_norm = [sb(f"y_norm{L}", [P, NT, HEADS, HD]) for L in range(2)]
        yT = [sb(f"yT{L}", [P, T]) for L in range(2)]
        h3 = sb("h3", [P, T])

        X1 = sb("X1", [P, TILES, C])
        XF = sb("XF", [P, TILES, C])
        H3 = [sb(f"H3_{part}", [P, TILES * P], F32R) for part in ("high", "low")]
        LG = sb("LG", [P, TILES, E])
        MOD = sb("MOD", [P, B, 6, C])

        top = sb("top", [P, TILES, TOPK_W])
        top_i = sb("top_i", [P, TILES, TOPK_W], U32)
        top_f = sb("top_f", [P, TILES, 2])
        iota_e = sb("iota_e", [P, E])
        t_dif = sb("t_dif", [P, TILES, 1])
        t_exp = sb("t_exp", [P, TILES, 1])
        t_sum = sb("t_sum", [P, TILES, 1])
        w_top = sb("w_top", [P, 2, TILES, 1])
        pick = sb("pick", [P, 2, TILES, E])
        EW = sb("EW", [P, TILES, E])
        ewT = sb("ewT", [E, TILES * P])
        b1_e = [sb(f"b1_e{n}", [P, NJ]) for n in range(2)]
        W1 = [sb(f"W1_{n}", [P, DFF]) for n in range(2)]
        W2 = [sb(f"W2_{n}", [P, NJ, C]) for n in range(2)]
        NCH = TILES * P // 512
        W1p = [[sb(f"W1_{part}{n}", [P, DFF], F32R) for part in ("high", "low")] for n in range(2)]
        W2p = [[sb(f"W2_{part}{n}", [P, NJ, C], F32R) for part in ("high", "low")] for n in range(2)]
        PRODUCTS = [(0, 0), (0, 1), (1, 0)]
        HALF_T = TILES * P // 2
        moeT = [v_pad[n][:, :, :, :].rearrange("p t h w -> p (t h w)") for n in range(2)]
        weighted = [rest[n][:, :, :].rearrange("p n t -> p (n t)") for n in range(2)]
        gate_diag = [xn[b // NT][:, b % NT, :] for b in range(B)]
        ew_bc = probs[1][:, :, :, :].rearrange("p (n j) t q -> p n (j t q)", n=2)
        hid = probs[0][:, :, :, :].rearrange("p j t q -> p j (t q)")
        hidp = [[stacked[L][h][:, :, :, :].rearrange("p (j a) b t -> p j (a b t)", j=NJ).bitcast(F32R) for h in range(2)]
                for L in range(2)]

        bank = [pb(f"bank{n}", [P, 512]) for n in range(8)]
        row_bank, col_bank, av_bank, max_bank = bank[0:2], bank[2:4], bank[4], bank[5]
        small = bank[6:8]
        out_banks = [bank[6], bank[7], bank[0], bank[1]]
        max_rows_ps = max_bank[:, :].bitcast(BF16)

        c_in = sem("c_in")
        early_in = sem("early_in")
        late_in = sem("late_in")
        consts = sem("consts")
        stacked_zero = sem("stacked_zero")
        dve_setup = sem("dve_setup")
        act_setup = sem("act_setup")
        pe_setup = sem("pe_setup")
        pool_setup = sem("pool_setup")
        mod_out = sem("mod_out")
        passed = sem("passed")
        x0_landed = sem("x0_landed")
        x_landed = sem("x_landed")
        mod0_landed = sem("mod0_landed")
        mod_landed = sem("mod_landed")
        stats_done = [sem(f"stats_done{n}") for n in range(4)]
        aggr_done = [sem(f"aggr_done{n}") for n in range(4)]
        eps_done = [sem(f"eps_done{n}") for n in range(4)]
        rstd_done = [sem(f"rstd_done{n}") for n in range(4)]
        norm_done = [sem(f"norm_done{n}") for n in range(4)]
        scale_done = [sem(f"scale_done{n}") for n in range(2)]
        shift_done = [sem(f"shift_done{n}") for n in range(2)]
        high_done = sems("high_done")
        mid_done = sems("mid_done")
        low_done = sems("low_done")
        half_landed = [sems(f"half{h}_landed") for h in range(2)]
        v_half_done = [sems(f"v_half{h}_done") for h in range(2)]
        small_full = sems("small_full")
        small_free = sems("small_free")
        rows_full = sem("rows_full")
        rows_free = sem("rows_free")
        cols_full = sem("cols_full")
        cols_free = sem("cols_free")
        max_split = sems("max_split")
        max_step = sems("max_step")
        maxT_full = sem("maxT_full")
        maxT_free = sem("maxT_free")
        shift_landed = sems("shift_landed")
        av_full = sem("av_full")
        y_sb_done = sem("y_sb_done")
        inv_done = sems("inv_done")
        y_norm_done = sems("y_norm_done")
        gabo_done = sem("gabo_done")
        x_gabo_done = sem("x_gabo_done")
        x1_done = sem("x1_done")
        xf_kept = sem("xf_kept")
        h3_free = sem("h3_free")
        top_step = sem("top_step")
        ew_exp = sem("ew_exp")
        ewT_full = sem("ewT_full")
        ewT_done = sem("ewT_done")
        ew_out = sem("ew_out")
        ew_landed = [sem(f"ew_landed{h}") for h in range(2)]
        b2_full = sem("b2_full")
        b2_kept = sem("b2_kept")
        weighted_done = sem("weighted_done")
        moe_T_full = sem("moe_T_full")
        w_landed = [sem(f"w_landed{n}") for n in range(2)]
        cols_e = sem("cols_e")
        up_full = sem("up_full")
        w_high = [sem(f"w_high{n}") for n in range(2)]
        w_split = [sem(f"w_split{n}") for n in range(2)]
        h3_high = sem("h3_high")
        hid_high = sem("hid_high")
        hid_low = sem("hid_low")
        down_full = sem("down_full")
        acc_done = sem("acc_done")
        gated = sem("gated")
        base_done = sem("base_done")
        diag_done = sem("diag_done")
        final = sem("final")
        stored = sem("stored")

        x_v = x_dram.rearrange("b (t p) c -> p (b t) c", p=P)
        out_v = out.rearrange("b (t p) c -> p (b t) c", p=P)
        w1_v = io["L0_ffn_W1"]
        w2_v = io["L0_ffn_W2"].rearrange("e (j p) c -> e p j c", p=P)
        EXPERT_LOOP = E // 2

        def row(v):
            return v.rearrange("(o c) -> o c", o=1)

        def x_of(b):
            return X1[:, bass.ds(b * NT, NT), :]

        def mod_of(b, m):
            return MOD[:, bass.ds(b, 1), m, :].to_broadcast([P, NT, C])

        def bcast(ap, n=NT):
            return ap[:, None, :].to_broadcast([P, n, C])

        def over_iterations(eng, body):
            for i in range(-1, LOOP[0]):
                body(i)
            with eng.Fori(LOOP[0], LOOP[1]) as i:
                body(i)
            for i in range(LOOP[1], B + 3):
                body(i)

        def over_experts(eng, body):
            body(0)
            with eng.Fori(1, EXPERT_LOOP) as m:
                body(m)

        block = ctx.enter_context(nc.Block())

        @block.sync
        def _(sp):
            def ones_rows(L):
                sp.wait_ge(stacked_zero, 2 * L + 2)
                for h in range(2):
                    sp.dma_start(stacked[L][h][SHIFT:P, :, 1, :], ones_bf[:, :, :]).then_inc(half_landed[h][L], 16)

            sp.dma_start(c_rows[:, :], io["L0_c"]).then_inc(c_in, 16)
            sp.dma_start(wmod[:, :], io["L0_wmod"]).then_inc(c_in, 16)
            early = [
                (w_in[0][:, 0:C], io["L0_attn_Wq"]), (w_in[0][:, C:2 * C], io["L0_attn_Wk"]),
                (w_in[0][:, 2 * C:3 * C], io["L0_attn_Wv"]),
                (qk_rows[0:1, :], row(io["L0_attn_bq"])), (qk_rows[1:2, :], row(io["L0_attn_bk"])),
                (qk_rows[2:4, :], io["L0_ffn_b_qkv"][0:2 * C].rearrange("(r c) -> r c", r=2)),
            ]
            assert len(early) == EARLY
            for dst, src in early:
                sp.dma_start(dst, src).then_inc(early_in, 16)
            sp.dma_start(X1[:, 0:NT, :], x_v[:, 0:NT, :]).then_inc(x0_landed, 16)
            sp.wait_ge(dve_setup, SETUP_MOD)
            sp.dma_start(mod_dram, mod[:, :, :].rearrange("b m c -> b (m c)")).then_inc(mod_out, 16)
            sp.wait_ge(consts, CONSTS)
            ones_rows(0)
            sp.wait_ge(mod_out, 16)
            for b in range(B):
                sp.dma_start(MOD[:, b, :, :].rearrange("p m c -> p (m c)"),
                             mod_dram[b:b + 1, :].to_broadcast([P, 6 * C])).then_inc(mod_landed if b else mod0_landed, 16)
            sp.dma_start(X1[:, NT:TILES, :], x_v[:, NT:TILES, :]).then_inc(x_landed, 16)

            def stack(L, b, h):
                at_least(sp, low_done[L], b + 1)
                if not isinstance(b, int) or b > 0:
                    sp.wait_ge(cols_full, 4 * place_of(L, b - 1, 2 * h + 1) + 4)
                for n, (qp, kp) in enumerate(PAIRS):
                    src = parts[L][64 * h:64 * h + 64, qp:4 + kp:3 + kp - qp, :]
                    dst = stacked[L][h][HD * n:HD * (n + 1), :, :, :]
                    sp.dma_start(dst, src).then_inc(half_landed[h][L], 16)

            def body(i):
                for turn in range(TURNS):
                    if turn == 2 and live(i - 2):
                        stack(1, i - 2, 1)
                    if turn == 3 and live(i + 1):
                        stack(0, i + 1, 0)
                    if turn == 5 and is_first(i, -1):
                        ones_rows(1)
                    if turn == 6 and live(i - 1):
                        stack(1, i - 1, 0)
                    if turn == 6 and live(i + 1):
                        stack(0, i + 1, 1)

            def load_weights(m, n):
                at_least(sp, w_split[n], m * 2)
                sp.dma_start(W1[n][:, :], w1_v[bass.ds(m * 2 + n, 1)].rearrange("o p f -> (o p) f")).then_inc(w_landed[n], 16)
                sp.dma_start(W2[n][:, :, :], w2_v[bass.ds(m * 2 + n, 1)].rearrange("o p j c -> (o p) j c")).then_inc(w_landed[n], 16)
            load_weights(0, 0)
            load_weights(0, 1)

            over_iterations(sp, body)

            sp.wait_ge(ewT_done, TILES // 4)
            sp.dma_start(ew_dram, ewT[:, :]).then_inc(ew_out, 16)
            sp.wait_ge(ew_out, 16)

            def load_experts(m):
                for n in range(2):
                    e = m * 2 + n
                    if not isinstance(m, int):
                        load_weights(m, n)
                    for h in range(2):
                        at_least(sp, weighted_done, (e - 1) * NCH + 2 * h + 2)
                        sp.dma_start(ew_bc[:, h, :], ew_dram[bass.ds(e, 1), HALF_T * h:HALF_T * (h + 1)].to_broadcast([P, HALF_T])
                                     ).then_inc(ew_landed[h], 16)
            over_experts(sp, load_experts)
            for ch in range(NCH):
                sp.wait_ge(final, ch + 1)
                sp.dma_start(out_v[:, 4 * ch:4 * ch + 4, :], X1[:, 4 * ch:4 * ch + 4, :]).then_inc(stored, 16)
            sp.wait_ge(stored, 16 * NCH)

        @block.gpsimd
        def _(pool):
            pool.memset(zeros[:, :], 0.0).then_inc(pool_setup, 1)
            pool.wait_ge(pool_setup, 1)
            pool.affine_select(out=ident[:, :], in_=zeros[:, :], compare_op=ALU.not_equal, fill=1.0, base=0,
                               pattern=[[-1, P]], channel_multiplier=1).then_inc(pool_setup, 1)
            pool.memset(eps[:, :], EPS).then_inc(consts, 1)
            pool.memset(minus_half[:, :], -0.5).then_inc(consts, 1)
            pool.memset(ones_bf[:, :, :], 1.0).then_inc(consts, 1)
            pool.iota(iota_e[:, :], pattern=[[1, E]], base=0, channel_multiplier=0,
                      allow_small_or_imprecise_dtypes=True).then_inc(consts, 1)
            pool.wait_ge(pool_setup, 2)
            pool.tensor_copy(ident_bf[:, :], ident[:, :]).then_inc(consts, 1)
            pool.affine_select(out=mask_qk[:, :], in_=zeros[:, :], compare_op=ALU.is_ge, fill=MASKED, base=0,
                               pattern=[[-1, P]], channel_multiplier=1).then_inc(consts, 1)
            pool.affine_select(out=mask_kq[:, :], in_=zeros[:, :], compare_op=ALU.is_ge, fill=MASKED, base=0,
                               pattern=[[1, P]], channel_multiplier=-1).then_inc(consts, 1)
            for L in range(2):
                pool.memset(v_pad[L][:, :, :, :], 0.0).then_inc(pool_setup, 1)
            pool.wait_ge(pool_setup, 4)
            for L in range(2):
                pool.memset(v_pad[L][:, :, :, HD:HD + 1], 1.0).then_inc(consts, 1)

            pool.sem_inc(h3_free, 1)

            def alone(s, value):
                pool.wait_ge(s, value)
                pool.sem_inc(passed, 1)

            def rstd_of(n, b):
                pool.wait_ge(aggr_done[n], 2 * b + 2)
                pool.tensor_tensor(var_eps[:, n, :], mean_var[:, n, :, 1], eps[:, :], ALU.add).then_inc(eps_done[n], 1)
                pool.wait_ge(eps_done[n], b + 1)
                pool.tensor_tensor(rstd[:, n, :], var_eps[:, n, :], minus_half[:, :], ALU.pow).then_inc(rstd_done[n], 1)

            def modulate(n, b, m, dst):
                pool.wait_ge(norm_done[n], 2 * b + 2)
                pool.tensor_tensor(xm[n][:, :, :], xn[n][:, :, :], mod_of(b, m + 1), ALU.mult).then_inc(scale_done[n], 1)
                pool.wait_ge(scale_done[n], b + 1)
                pool.tensor_tensor(dst[:, :, :], xm[n][:, :, :], mod_of(b, m), ALU.add).then_inc(shift_done[n], 1)

            def low(L, b):
                pool.wait_ge(mid_done[L], b + 1)
                pool.tensor_tensor(parts[L][:, 2:6:3, :], rest[L][:, :, :], parts[L][:, 1:5:3, :],
                                   ALU.subtract).then_inc(low_done[L], 1)

            def v_half(L, b, h, i):
                if not isinstance(b, int) or b > 0:
                    pool.wait_ge(av_full, place_of(L, b - 1, 2 * h + 1) + 1)
                alone(small_free[L], bank_place(L, i, "v"))
                hs = slice(SLOTS * h, SLOTS * (h + 1))
                pool.tensor_copy(v_pad[L][:, :, hs, 0:HD],
                                 v_flat[L][:, :, :].rearrange("p t (h d) -> p t h d", d=HD)[:, :, hs, :]).then_inc(v_half_done[h][L], 1)

            def body(i):
                for turn in range(TURNS):
                    if turn == 0:
                        if live(i + 1):
                            rstd_of(0, i + 1)
                        if live(i - 1):
                            b = i - 1
                            if is_first(i, 1):
                                pool.wait_ge(late_in, 16 * LATE)
                            pool.tensor_tensor(gabo[:, :], MOD[:, bass.ds(b, 1), GA, :].rearrange("p o c -> p (o c)"), bo_bc[0][:, :], ALU.mult).then_inc(gabo_done, 1)
                            pool.wait_ge(gabo_done, b + 1)
                            pool.tensor_tensor(x_gabo[:, :, :], x_of(b), bcast(gabo[:, :]), ALU.add).then_inc(x_gabo_done, 1)
                        if live(i + 1):
                            if is_first(i, -1):
                                pool.wait_ge(mod0_landed, 16)
                            if is_first(i, 0):
                                pool.wait_ge(mod_landed, 16 * (B - 1))
                            modulate(0, i + 1, SA, h_a)
                        if live(i):
                            v_half(0, i, 1, i - 1)
                    if turn == 1 and live(i - 1):
                        b = i - 1
                        rstd_of(1, b)
                        modulate(1, b, SB_, xf)
                    if turn == 2:
                        if live(i - 1):
                            b = i - 1
                            rstd_of(2, b)
                            pool.wait_ge(shift_done[1], b + 1)
                            pool.tensor_tensor(XF[:, bass.ds(b * NT, NT), :], xf[:, :, :], bcast(bo_bc[1][:, :]),
                                               ALU.add).then_inc(xf_kept, 1)
                    if turn == 3:
                        if live(i + 1):
                            low(0, i + 1)
                        if live(i - 2):
                            v_half(1, i - 2, 1, i - 1)
                    if turn == 4 and live(i + 1):
                        v_half(0, i + 1, 0, i)
                    if turn == 5:
                        if live(i - 1):
                            low(1, i - 1)
                    if turn == 6 and live(i - 3):
                        rstd_of(3, i - 3)
                    if turn == 7:
                        if live(i - 1):
                            v_half(1, i - 1, 0, i)
                        if live(i - 3):
                            alone(small_free[1], bank_place(1, i, "h3T"))
                            high, low_ = (H3[part][:, bass.ds((i - 3) * T, T)] for part in range(2))
                            pool.tensor_copy(high, h3[:, :]).then_inc(h3_high, 1)
                            pool.wait_ge(h3_high, i - 2)
                            pool.tensor_tensor(low_, h3[:, :], high, ALU.subtract).then_inc(h3_free, 1)
                for n in range(2):
                    if is_first(i, B + n):
                        split_expert(0, n)

            def split_expert(m, n):
                at_least(pool, down_full, (m * 2 + n - 1) * NCH)
                alone(w_landed[n], m * 32 + 32)
                pool.tensor_copy(W1p[n][0][:, :], W1[n][:, :]).then_inc(w_high[n], 1)
                pool.tensor_copy(W2p[n][0][:, :, :], W2[n][:, :, :]).then_inc(w_high[n], 1)
                pool.wait_ge(w_high[n], m * 2 + 2)
                pool.tensor_tensor(W1p[n][1][:, :], W1[n][:, :], W1p[n][0][:, :], ALU.subtract).then_inc(w_split[n], 1)
                pool.tensor_tensor(W2p[n][1][:, :, :], W2[n][:, :, :], W2p[n][0][:, :, :], ALU.subtract).then_inc(w_split[n], 1)

            over_iterations(pool, body)

            pool.wait_ge(small_free[1], bank_place(1, B + 2, "wo"))
            for ch in range(NCH):
                tiles = slice(4 * ch, 4 * ch + 4)
                f = XF[:, tiles, :].rearrange("p (b t) c -> p b t c", t=NT)
                g = MOD[:, 2 * ch:2 * ch + 2, GB:GB + 1, :].to_broadcast([P, 2, NT, C])
                pool.tensor_tensor(f, f, g, ALU.mult).then_inc(gated, 1)
                pool.wait_ge(gated, ch + 1)
                pool.tensor_tensor(X1[:, tiles, :], X1[:, tiles, :], XF[:, tiles, :], ALU.add).then_inc(base_done, 1)
            for b in range(B):
                pool.tensor_tensor(gate_diag[b], ident[:, :], MOD[:, b, GB, :], ALU.mult).then_inc(diag_done, 1)
            with pool.Fori(1, EXPERT_LOOP) as m:
                for n in range(2):
                    split_expert(m, n)

        @block.scalar
        def _(act):
            act.wait_ge(c_in, 32)
            act.activation(silu_e[:, :], c_rows[:, :], ACT.Exp, scale=-1.0).then_inc(act_setup, 1)
            late = [
                (w_in[1][:, :], io["L0_ffn_w_qkv"]),
                (vec_rows[BV0:BV0 + 1, :], row(io["L0_attn_bv"])),
                (vec_rows[BV1:BV1 + 1, :], row(io["L0_ffn_b_qkv"][2 * C:3 * C])),
                (vec_rows[G1:G1 + 1, :], row(io["L0_ffn_ln1_g"])), (vec_rows[B1_:B1_ + 1, :], row(io["L0_ffn_ln1_b"])),
                (vec_rows[G2:G2 + 1, :], row(io["L0_ffn_ln2_g"])), (vec_rows[B2_:B2_ + 1, :], row(io["L0_ffn_ln2_b"])),
                (vec_rows[NV:NV + E * NJ, :], io["L0_ffn_b1"].rearrange("e (j p) -> (e j) p", p=P)),
                (w_out[0][:, :], io["L0_attn_Wo"]), (w_out[1][:, :], io["L0_ffn_w_o"]),
                (gate_w[:, :], io["L0_ffn_gate_w"]), (b2_rows[:, :], io["L0_ffn_b2"]),
                (gate_b[:, :], row(io["L0_ffn_gate_b"]).to_broadcast([P, E])),
                (bo_bc[0][:, :], row(io["L0_attn_bo"]).to_broadcast([P, C])),
                (bo_bc[1][:, :], row(io["L0_ffn_b_o"]).to_broadcast([P, C])),
            ]
            assert len(late) == LATE
            act.wait_ge(pe_setup, 1)
            act.activation(silu_cT[:, :], max_bank[:, 256:256 + B], ACT.Copy).then_inc(act_setup, 1)
            for dst, src in late:
                act.dma_start(dst, src).then_inc(late_in, 16)
            act.wait_ge(pe_setup, 3)
            act.activation(qk_bias[:, :], max_bank[:, 0:4], ACT.Copy).then_inc(act_setup, 1)
            act.wait_ge(act_setup, 3)

            def vectors_out():
                act.wait_ge(pe_setup, 4)
                act.activation(vec[:, :], max_bank[:, 64:64 + NV + E * NJ], ACT.Copy).then_inc(act_setup, 1)
                act.wait_ge(act_setup, 4)

            def exps(i, turn, c):
                L, b, g = group_at(i, turn)
                if not live(b):
                    return
                n = 4 * place_of(L, b, g) + c
                act.wait_ge(cols_full, n + 1)
                width = [T + P, 2 * T][L]
                p = probs[probs_of(L, b, g)][:, c, :, :].rearrange("p t q -> p (t q)")
                act.activation(p[:, 0:width], col_bank[c % 2][:, 0:width], ACT.Exp, scale=SCALE).then_inc(cols_free, 1)

            def max_to_rows(i, turn):
                L, b, g = group_at(i, turn)
                if not live(b):
                    return
                n = place_of(L, b, g)
                act.wait_ge(maxT_full, n + 1)
                at_least(act, shift_landed[probs_of(L, b, g)], 16 * pair_of(L, b, g))
                act.activation(max_rows[probs_of(L, b, g)][:, :], max_rows_ps[0:2 * GH, 0:T], ACT.Copy).then_inc(maxT_free, 1)

            def shift_rows(i, turn):
                L, b, g = group_at(i, turn)
                if not live(b):
                    return
                h, s = g // 2, GH * (g % 2)
                act.wait_ge(maxT_free, place_of(L, b, g) + 1)
                dst = stacked[L][h][SHIFT:P, s:s + GH, 0, :]
                act.dma_start(dst, max_rows[probs_of(L, b, g)][:, :]).then_inc(shift_landed[probs_of(L, b, g)], 16)

            def y_out(i, turn):
                L, b, g = group_at(i, turn)
                if not live(b):
                    return
                n = place_of(L, b, g)
                act.wait_ge(av_full, n + 1)
                act.activation(y_sb[L][:, :], av_bank[:, 0:T], ACT.Copy).then_inc(y_sb_done, 1)

            def hT_out(L, b, i):
                act.wait_ge(small_full[L], bank_place(L, i, "xT"))
                if L == 0:
                    act.activation(hT[0][:, :], small[0][:, 0:T], ACT.Copy).then_inc(small_free[0], 1)
                else:
                    act.activation(hT[1][:, :], small[1][:, 0:T], ACT.Identity, bias=vec[:, B1_:B1_ + 1],
                                   scale=vec[:, G1:G1 + 1]).then_inc(small_free[1], 1)

            def high(L, b, i):
                act.wait_ge(small_full[L], bank_place(L, i, "qk"))
                at_least(act, half_landed[1][L], 16 * (6 * b + 1))
                for n in range(2):
                    act.activation(parts[L][:, 3 * n, :], small[L][:, T * n:T * (n + 1)], ACT.Identity,
                                   bias=qk_bias[:, 2 * L + n:2 * L + n + 1]).then_inc(high_done[L], 1)

            def mid(L, b, i):
                act.wait_ge(small_free[L], bank_place(L, i, "qk"))
                act.activation(parts[L][:, 1:5:3, :], rest[L][:, :, :], ACT.Copy).then_inc(mid_done[L], 1)

            def v_out(L, b, i):
                act.wait_ge(small_full[L], bank_place(L, i, "v"))
                at_least(act, v_half_done[1][L], b)
                act.activation(v_flat[L][:, :, :].rearrange("p t c -> p (t c)"), small[L][:, 0:T], ACT.Copy).then_inc(small_free[L], 1)

            def yT_out(L, b, i):
                act.wait_ge(small_full[L], bank_place(L, i, "y2T"))
                act.activation(yT[L][:, :], small[L][:, 0:T], ACT.Identity,
                               bias=vec[:, BV0 + L:BV0 + L + 1]).then_inc(small_free[L], 1)

            def body(i):
                for turn in range(TURNS):
                    for c in range(GH):
                        exps(i, turn, c)
                        if is_first(i, -1) and (turn, c) == (5, 1):
                            vectors_out()
                        if c == Y_OUT_AT:
                            y_out(i, turn - 1)
                        if c == MAX_AT:
                            max_to_rows(i, turn + 2)
                            shift_rows(i, turn + 2)
                        at = (turn, c)
                        if at == ACT_AT["yT0"] and live(i - 1):
                            yT_out(0, i - 1, i)
                        if at == ACT_AT["hT0"] and live(i + 1):
                            hT_out(0, i + 1, i)
                        if at == ACT_AT["yT1"] and live(i - 3):
                            yT_out(1, i - 3, i)
                        if at == ACT_AT["high0"] and live(i + 1):
                            high(0, i + 1, i)
                        if at == ACT_AT["mid0"] and live(i + 1):
                            mid(0, i + 1, i)
                        if at == ACT_AT["v0"] and live(i + 1):
                            v_out(0, i + 1, i)
                        if at == ACT_AT["h3"] and live(i - 3):
                            act.wait_ge(small_full[1], bank_place(1, i, "h3T"))
                            at_least(act, h3_free, i - 2)
                            act.activation(h3[:, :], small[1][:, 0:T], ACT.Identity, bias=vec[:, B2_:B2_ + 1],
                                           scale=vec[:, G2:G2 + 1]).then_inc(small_free[1], 1)
                        if at == ACT_AT["hT1"] and live(i - 1):
                            hT_out(1, i - 1, i)
                        if at == ACT_AT["high1"] and live(i - 1):
                            high(1, i - 1, i)
                        if at == ACT_AT["mid1"] and live(i - 1):
                            mid(1, i - 1, i)
                        if at == ACT_AT["v1"] and live(i - 1):
                            v_out(1, i - 1, i)

            over_iterations(act, body)

            act.wait_ge(top_step, TOP_DIF)
            act.activation(t_exp[:, :, :], t_dif[:, :, :], ACT.Exp).then_inc(ew_exp, 1)

            def ewT_out():
                for q in range(TILES // 4):
                    act.wait_ge(ewT_full, q + 1)
                    act.activation(ewT[:, 512 * q:512 * q + 512], small[q % 2][0:E, :], ACT.Copy).then_inc(ewT_done, 1)

            def relus(m):
                for n in range(2):
                    e = m * 2 + n
                    for ch in range(NCH):
                        for j in range(NJ):
                            act.wait_ge(up_full, (e * NCH + ch) * NJ + j + 1)
                            if ch == 0 and j == 0:
                                act.wait_ge(cols_e, e + 1)
                            at_least(act, hid_low, (e * NCH + ch - 1) * NJ + j + 1)
                            act.activation(hid[:, j, :], bank[j][:, :], ACT.Relu, bias=b1_e[n][:, j:j + 1])
                            if j == 0:
                                at_least(act, down_full, e * NCH + ch - 1)
                            act.activation(hidp[ch % 2][0][:, j, :], bank[j][:, :], ACT.Relu,
                                           bias=b1_e[n][:, j:j + 1]).then_inc(hid_high, 1)
                        if is_first(m, 0) and n == 0 and ch == 0:
                            ewT_out()

            over_experts(act, relus)

        @block.vector
        def _(dve):
            steps = [0]

            def link(ins):
                steps[0] += 1
                ins.then_inc(dve_setup, 1)
                dve.wait_ge(dve_setup, steps[0])

            def clear(L, h):
                dve.memset(stacked[L][h][:, :, :, :], 0.0).then_inc(stacked_zero, 1)

            def permuted(dst, src):
                return (dst.rearrange("p (a d s) -> p a s d", a=2, d=HD), src.rearrange("p (a s d) -> p a s d", a=2, s=SLOTS))

            def permute_w(L):
                for n in range(2):
                    for a in range(2):
                        o, s = permuted(w_qk[L][:, n, :], w_in[L][:, C * n:C * (n + 1)])
                        ins = dve.tensor_copy(o[:, a], s[:, a])
                return ins
            clear(0, 0)
            dve.wait_ge(c_in, 32)
            dve.wait_ge(act_setup, 1)
            link(dve.tensor_scalar(silu_r[:, :], silu_e[:, :], 1.0, None, ALU.add))
            link(dve.reciprocal(silu_e[:, :], silu_r[:, :]))
            link(dve.tensor_tensor(silu_c[:, :], c_rows[:, :], silu_e[:, :], ALU.mult))
            assert steps[0] == SETUP_SILU
            dve.wait_ge(early_in, 16 * EARLY)
            permute_w(0)
            for a in range(2):
                o, s = permuted(qk_rows_p[:, :], qk_rows[:, :])
                ins = dve.tensor_copy(o[:, a], s[:, a])
            link(ins)
            assert steps[0] == SETUP_QK
            dve.wait_ge(pe_setup, 2)
            m2 = mod[:, :, :].rearrange("b m c -> b (m c)")
            dve.tensor_copy(m2[:, 0:512], bank[0][0:B, :])
            link(dve.tensor_copy(m2[:, 512:768], bank[1][0:B, 0:256]))
            for m in (CA, CB):
                link(dve.tensor_scalar(mod[:, m, :], mod[:, m, :], 1.0, None, ALU.add))
            gates = mod[:, GA:GB + 1:GB - GA, :]
            link(dve.tensor_scalar(mod_sign[:, :, :], gates, 0.0, 2.0, ALU.is_ge, ALU.mult))
            link(dve.tensor_scalar(mod_sign[:, :, :], mod_sign[:, :, :], -1.0, None, ALU.add))
            link(dve.scalar_tensor_tensor(out=mod_abs[:, :, :], in0=gates, scalar=-1.0, in1=gates, op0=ALU.mult, op1=ALU.max))
            link(dve.scalar_tensor_tensor(out=gates, in0=mod_abs[:, :, :], scalar=0.25, in1=mod_sign[:, :, :],
                                          op0=ALU.max, op1=ALU.mult))
            assert steps[0] == SETUP_MOD
            clear(0, 1)

            def second_layer():
                for h in range(2):
                    clear(1, h)
                dve.wait_ge(late_in, 16 * LATE)
                link(permute_w(1))
                assert steps[0] == SETUP_QK1

            def alone(s, value):
                dve.wait_ge(s, value)
                dve.sem_inc(passed, 1)

            def x_tile(b, t):
                return X1[:, bass.ds(b * NT + t, 1), :].rearrange("p o c -> p (o c)")

            def xf_tile(b, t):
                return xf[:, t, :]

            def xf2_tile(b, t):
                return XF[:, bass.ds(b * NT + t, 1), :].rearrange("p o c -> p (o c)")

            def norm_stats(n, b, src):
                for t in range(NT):
                    dve.bn_stats(stats[:, n, t, :], src(b, t)).then_inc(stats_done[n], 1)
                alone(stats_done[n], 2 * b + 2)
                for t in range(NT):
                    dve.bn_aggr(mean_var[:, n, t, :], stats[:, n, t, :]).then_inc(aggr_done[n], 1)

            def normalize(n, b, src):
                dve.wait_ge(rstd_done[n], b + 1)
                dve.wait_ge(aggr_done[n], 2 * b + 2)
                for t in range(NT):
                    dve.tensor_scalar(xn[n][:, t, :], src(b, t), mean_var[:, n, t, 0:1], rstd[:, n, t:t + 1],
                                      ALU.subtract, ALU.mult).then_inc(norm_done[n], 1)

            def row_max(i, turn, c):
                L, b, g = group_at(i, turn)
                if not live(b):
                    return
                n = 4 * place_of(L, b, g) + c
                dve.wait_ge(rows_full, n + 1)
                if c == 0:
                    at_least(dve, max_split[L], 2 * (4 * b + g))
                blocks, width = [(3, P), (2, T)][L]
                src = row_bank[c % 2][:, 0:blocks * width].rearrange("p (a k) -> p a k", a=blocks)
                dve.tensor_reduce(neg_max[L][:, :, c], src, AX.X, ALU.max, negate=True).then_inc(rows_free, 1)

            def split_max(i, turn):
                L, b, g = group_at(i, turn)
                if not live(b):
                    return
                n = 4 * b + g
                dve.wait_ge(rows_free, 4 * place_of(L, b, g) + 4)
                if L == 0:
                    dve.tensor_tensor(neg_max[0][:, 1, :], neg_max[0][:, 1, :], neg_max[0][:, 2, :],
                                      ALU.min).then_inc(max_step[0], 1)
                    dve.wait_ge(max_step[0], n + 1)
                if not isinstance(b, int) or n > 0:
                    pb_, pg = (b, g - 1) if g > 0 else (b - 1, GROUPS - 1)
                    dve.wait_ge(maxT_full, place_of(L, pb_, pg) + 1)
                dve.tensor_copy(max_parts[L][:, :, 0, :], neg_max[L][:, 0:2, :]).then_inc(max_split[L], 1)
                dve.wait_ge(max_split[L], 2 * n + 1)
                dve.tensor_tensor(max_parts[L][:, :, 1, :], neg_max[L][:, 0:2, :], max_parts[L][:, :, 0, :],
                                  ALU.subtract).then_inc(max_split[L], 1)

            def y_normalize(i, turn):
                L, b, g = group_at(i, turn)
                if not live(b):
                    return
                n = 4 * b + g
                dve.wait_ge(small_full[L], bank_place(L, i, "yT", g))
                ps = small[L][:, 0:T].rearrange("p (t c w) -> p t c w", t=NT, c=GH)
                dve.reciprocal(y_inv[L][:, :, :, :], ps[:, :, :, HD:HD + 1]).then_inc(inv_done[L], 1)
                dve.wait_ge(inv_done[L], n + 1)
                ins = None
                for t in range(NT):
                    ins = dve.tensor_tensor(y_norm[L][:, t, GH * g:GH * g + GH, :], ps[:, t, :, 0:HD],
                                            y_inv[L][:, t, :, :].to_broadcast([P, GH, HD]), ALU.mult)
                    if t == NT - 1:
                        ins.then_inc(small_free[L], 1)

            def rest_of(L, b, i):
                dve.wait_ge(high_done[L], 2 * b + 2)
                at_least(dve, low_done[L], b)
                for n in range(2):
                    ins = dve.scalar_tensor_tensor(out=rest[L][:, n, :], in0=small[L][:, T * n:T * (n + 1)],
                                                   scalar=qk_bias[:, 2 * L + n:2 * L + n + 1], in1=parts[L][:, 3 * n, :],
                                                   op0=ALU.add, op1=ALU.subtract)
                ins.then_inc(small_free[L], 1)

            def body(i):
                for turn in range(TURNS):
                    for c in range(GH):
                        row_max(i, turn + 3, c)
                        at = (turn, c)
                        if c == Y_NORM_AT:
                            y_normalize(i, turn - 2)
                        if at == DVE_AT["stats0"] and live(i + 1):
                            if is_first(i, -1):
                                dve.wait_ge(x0_landed, 16)
                            if is_first(i, 0):
                                dve.wait_ge(x_landed, 16)
                            norm_stats(0, i + 1, x_tile)
                        if at == DVE_AT["norm0"] and live(i + 1):
                            at_least(dve, scale_done[0], i + 1)
                            normalize(0, i + 1, x_tile)
                        if at == DVE_AT["x1"] and live(i - 1):
                            b = i - 1
                            dve.wait_ge(small_full[0], bank_place(0, i, "wo"))
                            if is_first(i, 1):
                                dve.wait_ge(mod_landed, 16 * (B - 1))
                            dve.tensor_tensor(attn_g[:, :, :], small[0][:, 0:T].rearrange("p (t c) -> p t c", t=NT),
                                              mod_of(b, GA), ALU.mult).then_inc(small_free[0], 1)
                            dve.wait_ge(small_free[0], bank_place(0, i, "wo"))
                            dve.wait_ge(x_gabo_done, b + 1)
                            dve.tensor_tensor(x_of(b), attn_g[:, :, :], x_gabo[:, :, :], ALU.add).then_inc(x1_done, 1)
                            alone(x1_done, b + 1)
                            norm_stats(1, b, x_tile)
                        if at == DVE_AT["norm1"] and live(i - 1):
                            at_least(dve, scale_done[1], i - 1)
                            normalize(1, i - 1, x_tile)
                        if at == DVE_AT["rest0"] and live(i + 1):
                            rest_of(0, i + 1, i)
                        if at == DVE_AT["stats2"] and live(i - 1):
                            dve.wait_ge(shift_done[1], i)
                            norm_stats(2, i - 1, xf_tile)
                        if at == DVE_AT["norm2"] and live(i - 1):
                            normalize(2, i - 1, xf_tile)
                        if at == DVE_AT["rest1"] and live(i - 1):
                            rest_of(1, i - 1, i)
                        if at == DVE_AT["xf2"] and live(i - 3):
                            b = i - 3
                            dve.wait_ge(small_full[1], bank_place(1, i, "wo"))
                            dve.wait_ge(xf_kept, b + 1)
                            rows = XF[:, bass.ds(b * NT, NT), :]
                            dve.tensor_tensor(rows, rows, small[1][:, 0:T].rearrange("p (t c) -> p t c", t=NT),
                                              ALU.add).then_inc(small_free[1], 1)
                            alone(small_free[1], bank_place(1, i, "wo"))
                            norm_stats(3, b, xf2_tile)
                        if at == DVE_AT["norm3"] and live(i - 3):
                            normalize(3, i - 3, xf2_tile)
                        if at == DVE_AT["logits"] and live(i - 3):
                            b = i - 3
                            dve.wait_ge(small_full[1], bank_place(1, i, "gate"))
                            dve.tensor_tensor(LG[:, bass.ds(b * NT, NT), :],
                                              small[1][:, 0:NT * E].rearrange("p (t e) -> p t e", t=NT),
                                              gate_b[:, None, :].to_broadcast([P, NT, E]), ALU.add).then_inc(small_free[1], 1)
                    if turn == 3 and is_first(i, -1):
                        second_layer()
                    split_max(i, turn + 3)

            over_iterations(dve, body)

            made = [0]

            def then(ins):
                made[0] += 1
                ins.then_inc(top_step, 1)
                dve.wait_ge(top_step, made[0])
            dve.wait_ge(consts, CONSTS)
            for n in range(2):
                dve.tensor_copy(b1_e[n][:, :], vec[:, n * NJ + NV:(n + 1) * NJ + NV]).then_inc(cols_e, 1)
            dve.wait_ge(small_free[1], bank_place(1, B + 2, "gate"))
            for t in range(TILES):
                ins = dve.max(top[:, t, :], LG[:, t, :])
            then(ins)
            for t in range(TILES):
                dve.max_index(top_i[:, t, :], top[:, t, :], LG[:, t, :])
            ins = dve.tensor_tensor(t_dif[:, :, :], top[:, :, 1:2], top[:, :, 0:1], ALU.subtract)
            then(ins)
            assert made[0] == TOP_DIF
            then(dve.tensor_copy(top_f[:, :, :], top_i[:, :, 0:2]))
            dve.wait_ge(ew_exp, 1)
            then(dve.tensor_scalar(t_sum[:, :, :], t_exp[:, :, :], 1.0, None, ALU.add))
            then(dve.reciprocal(w_top[:, 0, :, :], t_sum[:, :, :]))
            then(dve.tensor_tensor(w_top[:, 1, :, :], w_top[:, 0, :, :], t_exp[:, :, :], ALU.mult))
            iotas = iota_e[:, None, :].to_broadcast([P, TILES, E])
            for k in range(2):
                then(dve.tensor_tensor(pick[:, k, :, :], iotas, top_f[:, :, k:k + 1].to_broadcast([P, TILES, E]), ALU.is_equal))
                then(dve.tensor_tensor(pick[:, k, :, :], pick[:, k, :, :], w_top[:, k, :, :].to_broadcast([P, TILES, E]), ALU.mult))
            then(dve.tensor_tensor(EW[:, :, :], pick[:, 0, :, :], pick[:, 1, :, :], ALU.add))
            assert made[0] == TOP_ALL

            def b2_out():
                for ch in range(NCH):
                    dve.wait_ge(b2_full, ch + 1)
                    dve.tensor_copy(moeT[ch // 2][:, 512 * (ch % 2):512 * (ch % 2) + 512], small[ch % 2][:, :]).then_inc(b2_kept, 1)
                dve.wait_ge(b2_kept, NCH)

            def accumulate(e, n, ch):
                dve.wait_ge(down_full, e * NCH + ch + 1)
                if ch % 2 == 0:
                    dve.wait_ge(ew_landed[ch // 2], 16 * e + 16)
                cols = slice(512 * (ch % 2), 512 * (ch % 2) + 512)
                at_least(dve, acc_done, e * NCH + ch - 1)
                dve.tensor_tensor(weighted[ch % 2], bank[4 + ch % 2][:, :], ew_bc[:, ch // 2, cols],
                                  ALU.mult).then_inc(weighted_done, 1)
                dve.wait_ge(weighted_done, e * NCH + ch + 1)
                at_least(dve, acc_done, (e - 1) * NCH + ch + 1)
                dve.tensor_tensor(moeT[ch // 2][:, cols], moeT[ch // 2][:, cols], weighted[ch % 2], ALU.add).then_inc(acc_done, 1)

            def lows(m):
                for n in range(2):
                    e = m * 2 + n
                    if not is_first(m, 0):
                        dve.tensor_copy(b1_e[n][:, :], vec[:, bass.ds(e * NJ + NV, NJ)]).then_inc(cols_e, 1)
                    for ch in range(NCH):
                        for j in range(NJ):
                            dve.wait_ge(hid_high, (e * NCH + ch) * NJ + j + 1)
                            dve.tensor_tensor(hidp[ch % 2][1][:, j, :], hid[:, j, :], hidp[ch % 2][0][:, j, :],
                                              ALU.subtract).then_inc(hid_low, 1)
                        if is_first(m, 0) and n == 0 and ch == 0:
                            b2_out()
                        if ch > 0:
                            accumulate(e, n, ch - 1)
                        elif not isinstance(e, int) or e > 0:
                            accumulate(e - 1, 1 - n, NCH - 1)
            over_experts(dve, lows)
            for ch in range(NCH):
                if ch == 2:
                    accumulate(E - 1, 1, NCH - 1)
                dve.wait_ge(moe_T_full, ch + 1)
                dve.wait_ge(base_done, ch + 1)
                tiles = slice(4 * ch, 4 * ch + 4)
                dve.tensor_tensor(X1[:, tiles, :], X1[:, tiles, :], out_banks[ch][:, :].rearrange("p (t c) -> p t c", t=4),
                                  ALU.add).then_inc(final, 1)

        @block.tensor
        def _(pe):
            pe.wait_ge(pool_setup, 2)
            pe.wait_ge(dve_setup, SETUP_SILU)
            pe.transpose(max_bank[:, 256:256 + B], silu_c[:, :], ident[0:B, 0:B]).then_inc(pe_setup, 1)
            pe.wait_ge(act_setup, 2)
            pe.matmul(bank[0][0:B, :], silu_cT[:, :], wmod[:, 0:512], start=True, stop=True)
            pe.matmul(bank[1][0:B, 0:256], silu_cT[:, :], wmod[:, 512:768], start=True, stop=True).then_inc(pe_setup, 1)
            pe.wait_ge(dve_setup, SETUP_QK)
            pe.transpose(max_bank[:, 0:4], qk_rows_p[:, :], ident[0:4, 0:4]).then_inc(pe_setup, 1)
            pe.wait_ge(dve_setup, SETUP_QK + 1)
            pe.wait_ge(consts, CONSTS)

            def vectors():
                pe.wait_ge(late_in, 16 * LATE)
                pe.wait_ge(act_setup, 3)
                nv = NV + E * NJ
                pe.transpose(max_bank[:, 64:64 + nv], vec_rows[:, :], ident[0:nv, 0:nv]).then_inc(pe_setup, 1)

            def scores_rows(i, turn, c):
                L, b, g = group_at(i, turn)
                if not live(b):
                    return
                n = 4 * place_of(L, b, g) + c
                h, s = g // 2, GH * (g % 2) + c
                if c == 0 and g % 2 == 0:
                    pe.wait_ge(half_landed[h][L], 16 * (1 + 6 * (b + 1)))
                at_least(pe, rows_free, n - 1)
                q, k = stacked[L][h][0:SHIFT, s, 0, :], stacked[L][h][0:SHIFT, s, 1, :]
                ps = row_bank[c % 2]
                if L == 0:
                    pe.matmul(ps[:, 0:P], q[:, 0:P], k[:, 0:P], start=True, stop=True)
                    pe.matmul(ps[:, 0:P], ident_bf[:, :], mask_qk[:, :], start=False, stop=True, skip_group_check=True)
                    pe.matmul(ps[:, P:3 * P], q[:, P:T], k[:, :], start=True, stop=True)
                    ins = pe.matmul(ps[:, 2 * P:3 * P], ident_bf[:, :], mask_qk[:, :], start=False, stop=True,
                                    skip_group_check=True)
                else:
                    pe.matmul(ps[:, 0:T], q[:, 0:P], k[:, :], start=True, stop=True)
                    ins = pe.matmul(ps[:, T:2 * T], q[:, P:T], k[:, :], start=True, stop=True)
                ins.then_inc(rows_full, 1)

            def scores_cols(i, turn, c):
                L, b, g = group_at(i, turn)
                if not live(b):
                    return
                n = 4 * place_of(L, b, g) + c
                h, s = g // 2, GH * (g % 2) + c
                if c == 0:
                    pe.wait_ge(shift_landed[probs_of(L, b, g)], 16 * (pair_of(L, b, g) + 1))
                at_least(pe, cols_free, n - 1)
                q, k = stacked[L][h][:, s, 0, :], stacked[L][h][:, s, 1, :]
                ps = col_bank[c % 2]
                if L == 0:
                    pe.matmul(ps[:, 0:T], k[:, 0:P], q[:, :], start=True, stop=True)
                    pe.matmul(ps[:, 0:P], ident_bf[:, :], mask_kq[:, :], start=False, stop=True, skip_group_check=True)
                    pe.matmul(ps[:, T:T + P], k[:, P:T], q[:, P:T], start=True, stop=True)
                    ins = pe.matmul(ps[:, T:T + P], ident_bf[:, :], mask_kq[:, :], start=False, stop=True, skip_group_check=True)
                else:
                    pe.matmul(ps[:, 0:T], k[:, 0:P], q[:, :], start=True, stop=True)
                    ins = pe.matmul(ps[:, T:2 * T], k[:, P:T], q[:, :], start=True, stop=True)
                ins.then_inc(cols_full, 1)

            def max_transposes(i, turn):
                L, b, g = group_at(i, turn)
                if not live(b):
                    return
                n = place_of(L, b, g)
                pe.wait_ge(max_split[L], 2 * (4 * b + g) + 2)
                if is_first(n, 0):
                    pe.wait_ge(act_setup, 4)
                at_least(pe, maxT_free, n)
                for t in range(NT):
                    ins = pe.transpose(max_rows_ps[0:2 * GH, P * t:P * (t + 1)],
                                       max_parts[L][:, t, :, :].rearrange("p a c -> p (a c)"), ident_bf[:, :])
                ins.then_inc(maxT_full, 1)

            def weighted_values(i, turn):
                L, b, g = group_at(i, turn)
                if not live(b):
                    return
                n = place_of(L, b, g)
                pe.wait_ge(cols_free, 4 * n + 4)
                if g % 2 == 0:
                    pe.wait_ge(v_half_done[g // 2][L], b + 1)
                at_least(pe, y_sb_done, n)
                p = probs[probs_of(L, b, g)]
                for t in range(NT):
                    for c in range(GH):
                        ps = av_bank[VW * c:VW * (c + 1), 0:T]
                        v = v_pad[L][:, t, GH * g + c, :]
                        pc = p[:, c, :, :].rearrange("p t q -> p (t q)")
                        if L == 0 and t == 1:
                            ins = pe.matmul(ps[:, P:T], v, pc[:, T:T + P], start=False, stop=True,
                                            tile_position=(0, VW * c), skip_group_check=True)
                        else:
                            ins = pe.matmul(ps, v, pc[:, T * t:T * (t + 1)], start=(t == 0), stop=(t == 1),
                                            tile_position=(0, VW * c), skip_group_check=True)
                ins.then_inc(av_full, 1)

            def fill(L, place):
                if isinstance(place, int):
                    at_least(pe, small_free[L], place - 1)
                else:
                    pe.wait_ge(small_free[L], place - 1)

            def y_transposes(i, turn):
                L, b, g = group_at(i, turn)
                if not live(b):
                    return
                fill(L, bank_place(L, i, "yT", g))
                pe.wait_ge(y_sb_done, place_of(L, b, g) + 1)
                for t in range(NT):
                    ins = pe.transpose(small[L][:, P * t:P * (t + 1)], y_sb[L][:, P * t:P * (t + 1)], ident[:, :])
                ins.then_inc(small_full[L], 1)

            def tiles_T(L, src):
                for t in range(NT):
                    ins = pe.transpose(small[L][:, P * t:P * (t + 1)], src[:, t, :], ident[:, :])
                ins.then_inc(small_full[L], 1)

            def y2T(L, b):
                tiles_T(L, y_norm[L][:, :, :, :].rearrange("p t h d -> p t (h d)"))

            def project_y(L, b):
                for t in range(NT):
                    ins = pe.matmul(small[L][:, C * t:C * (t + 1)], yT[L][:, P * t:P * (t + 1)], w_out[L][:, :],
                                    start=True, stop=True)
                ins.then_inc(small_full[L], 1)

            def xT(L, b):
                if L == 0:
                    pe.wait_ge(shift_done[0], b + 1)
                    tiles_T(0, h_a)
                else:
                    pe.wait_ge(norm_done[2], 2 * b + 2)
                    tiles_T(1, xn[2])

            def project_qk(L, b):
                if L == 1 and is_first(b, 0):
                    pe.wait_ge(dve_setup, SETUP_QK1)
                for n in range(2):
                    ins = pe.matmul(small[L][:, T * n:T * (n + 1)], w_qk[L][:, n, :], hT[L][:, :], start=True, stop=True)
                ins.then_inc(small_full[L], 1)

            def project_v(L, b):
                for t in range(NT):
                    ins = pe.matmul(small[L][:, C * t:C * (t + 1)], hT[L][:, P * t:P * (t + 1)],
                                    w_in[L][:, 2 * C:3 * C], start=True, stop=True)
                ins.then_inc(small_full[L], 1)

            def h3T(L, b):
                pe.wait_ge(norm_done[3], 2 * b + 2)
                tiles_T(L, xn[3])

            def gate(L, b):
                for t in range(NT):
                    ins = pe.matmul(small[L][:, E * t:E * (t + 1)], h3[:, P * t:P * (t + 1)], gate_w[:, :],
                                    start=True, stop=True)
                ins.then_inc(small_full[L], 1)

            does = {"y2T": y2T, "wo": project_y, "xT": xT, "qk": project_qk, "v": project_v, "h3T": h3T, "gate": gate}
            steps = {step: (place, does[step[0]]) for step, place in PE_AT.items()}

            def body(i):
                for turn in range(TURNS):
                    for c in range(GH):
                        scores_cols(i, turn, c)
                        scores_rows(i, turn + 3, c)
                        at = (turn, c)
                        if c == YT_AT:
                            y_transposes(i, turn - 2)
                        if c == MAXT_AT:
                            max_transposes(i, turn + 2)
                        if c == AV_AT:
                            weighted_values(i, turn - 1)
                        if is_first(i, -1) and (turn, c) == (5, 0):
                            vectors()
                        for step, ((when, later), do) in steps.items():
                            if when == (turn, c) and live(i + later):
                                fill(step[1], bank_place(step[1], i, step[0]))
                                do(step[1], i + later)

            over_iterations(pe, body)

            def second_biases():
                pe.wait_ge(top_step, TOP_ALL)
                for q in range(TILES // 4):
                    at_least(pe, ewT_done, q - 1)
                    for k in range(4):
                        ins = pe.transpose(small[q % 2][0:E, P * k:P * (k + 1)], EW[:, 4 * q + k, :], ident[:, :])
                    ins.then_inc(ewT_full, 1)
                for ch in range(NCH):
                    if ch < 2:
                        pe.wait_ge(ewT_done, ch + TILES // 4 - 1)
                    else:
                        pe.wait_ge(b2_kept, ch - 1)
                    pe.matmul(small[ch % 2][:, :], b2_rows[:, :], ewT[:, 512 * ch:512 * ch + 512],
                              start=True, stop=True).then_inc(b2_full, 1)

            pe.wait_ge(h3_free, B + 1)

            def up(e, n, ch):
                for j in range(NJ):
                    at_least(pe, hid_high, (e * NCH + ch - 1) * NJ + j + 1)
                    for p, (wp, hp) in enumerate(PRODUCTS):
                        ins = pe.matmul(bank[j][:, :], W1p[n][wp][:, P * j:P * (j + 1)],
                                        H3[hp][:, 512 * ch:512 * (ch + 1)], start=(p == 0), stop=(p == 2))
                    ins.then_inc(up_full, 1)

            def down(e, n, ch):
                at_least(pe, weighted_done, e * NCH + ch - 1)
                pe.wait_ge(hid_low, (e * NCH + ch + 1) * NJ)
                for j in range(NJ):
                    for p, (wp, hp) in enumerate(PRODUCTS):
                        ins = pe.matmul(bank[4 + ch % 2][:, :], W2p[n][wp][:, j, :], hidp[ch % 2][hp][:, j, :],
                                        start=(j == 0 and p == 0), stop=(j == NJ - 1 and p == 2))
                ins.then_inc(down_full, 1)

            def experts(m):
                for n in range(2):
                    e = m * 2 + n
                    pe.wait_ge(w_split[n], m * 2 + 2)
                    for ch in range(NCH):
                        up(e, n, ch)
                        if is_first(m, 0) and n == 0 and ch == 0:
                            second_biases()
                        if ch > 0:
                            down(e, n, ch - 1)
                        elif not isinstance(e, int) or e > 0:
                            down(e - 1, 1 - n, NCH - 1)

            over_experts(pe, experts)

            def sums_back(ch):
                pe.wait_ge(acc_done, (E - 1) * NCH + ch + 1)
                for k in range(4):
                    n = 4 * (ch % 2) + k
                    ins = pe.matmul(out_banks[ch][:, P * k:P * (k + 1)], moeT[ch // 2][:, P * n:P * (n + 1)],
                                    gate_diag[2 * ch + k // NT], start=True, stop=True)
                ins.then_inc(moe_T_full, 1)

            pe.wait_ge(diag_done, B)
            for ch in range(2):
                sums_back(ch)
            down(E - 1, 1, NCH - 1)
            for ch in range(2, NCH):
                sums_back(ch)


_INS = ['L0_attn_x', 'L0_attn_Wq', 'L0_attn_bq', 'L0_attn_Wk', 'L0_attn_bk', 'L0_attn_Wv', 'L0_attn_bv',
        'L0_attn_Wo', 'L0_attn_bo', 'L0_ffn_ln1_g', 'L0_ffn_ln1_b', 'L0_ffn_w_qkv', 'L0_ffn_b_qkv', 'L0_ffn_w_o',
        'L0_ffn_b_o', 'L0_ffn_ln2_g', 'L0_ffn_ln2_b', 'L0_ffn_gate_w', 'L0_ffn_gate_b', 'L0_ffn_W1', 'L0_ffn_b1',
        'L0_ffn_W2', 'L0_ffn_b2', 'L0_c', 'L0_wmod']


def kernel(**inputs):
    import numpy as _np
    import concourse.bacc as _bacc
    from concourse import mybir as _mybir
    from concourse.bass_utils import run_bass_kernel_spmd as _run

    nc = _bacc.Bacc("TRN2", target_bir_lowering=False, num_devices=1)
    arrays, io = {}, {}
    for name in _INS:
        a = _np.ascontiguousarray(inputs[name])
        arrays[f"in_{name}"] = a
        io[name] = nc.dram_tensor(f"in_{name}", a.shape, _mybir.dt.from_np(a.dtype), kind="ExternalInput").ap()
    batches = inputs["L0_c"].shape[0]
    out = nc.dram_tensor("out_0", inputs["L0_attn_x"].shape, _mybir.dt.float32, kind="ExternalOutput").ap()
    mod_dram = nc.dram_tensor("mod_rows", (batches, inputs["L0_wmod"].shape[1]), _mybir.dt.float32, kind="Internal").ap()
    batches, tokens, _ = inputs["L0_attn_x"].shape
    experts = inputs["L0_ffn_gate_w"].shape[1]
    ew_dram = nc.dram_tensor("ew_rows", (experts, batches * tokens), _mybir.dt.float32, kind="Internal").ap()
    build(nc, io, out, mod_dram, ew_dram)
    r = _run(nc, [arrays], core_ids=[0])
    return r.results[0]["out_0"]
```
